# Optimizing a Trainium2 kernel written in Bass

```python
import numpy as np
import jax
import jax.numpy as jnp

def _softmax(x, axis=-1):
    return jax.nn.softmax(x, axis=axis)

def _gelu(x):
    return jax.nn.gelu(x, approximate=True)

def _silu(x):
    return jax.nn.silu(x)

def _sigmoid(x):
    return jax.nn.sigmoid(x)

def _layernorm(x, axis=-1, eps=1e-05):
    m = jnp.mean(x, axis=axis, keepdims=True)
    v = jnp.var(x, axis=axis, keepdims=True)
    return (x - m) / jnp.sqrt(v + eps)

def _scatter_add(tgt, idx, src, axis=0):
    return tgt.at[idx].add(src)

def _segment_sum(src, seg, n):
    return jax.ops.segment_sum(src, seg, n)
kernel_name = 'mk_xattn_seq_d2_seqx_r2_f2312b'

def setup_inputs(seed: int=0):
    np.random.seed(seed)
    _w = jnp.asarray

    def _rec_inputs():
        import jax
        import jax.numpy as jnp
        _rk = jax.random.key(seed)
        x = -0.000125 + 0.9999 * jax.random.normal(jax.random.fold_in(_rk, 1), (32, 256, 512), jnp.float32)
        _lenS = 256 - jax.random.randint(jax.random.fold_in(_rk, 7), (32,), 0, max(1, 256 // 4) + 1, jnp.int32)
        _lenS2 = 256 - jax.random.randint(jax.random.fold_in(_rk, 8), (32,), 0, max(1, 256 // 4) + 1, jnp.int32)
        _ctx_512P = jax.random.normal(jax.random.fold_in(_rk, 11), (32, 16, 256), jnp.float32)
        _ctx_512c = jax.random.dirichlet(jax.random.fold_in(_rk, 511), 0.3 * jnp.ones((16,), jnp.float32), (32, 256))
        _ctx_512t = jnp.einsum('bsk,bkd->bsd', _ctx_512c, _ctx_512P)
        _ctx_512t = _ctx_512t * jax.lax.rsqrt(jnp.mean(jnp.square(_ctx_512t)) + 1e-12) * 0.953939
        ctx_512 = 0.000227908 + 0.99994 * (_ctx_512t + 0.3 * jax.random.normal(jax.random.fold_in(_rk, 611), (32, 256, 256), jnp.float32))
        return (x, ctx_512)
    x, ctx_512 = _rec_inputs()

    def _L0_xattn_setup():
        import jax, jax.numpy as jnp
        import numpy as np
        B, T, E = (8, 2048, 512)
        M, L = (128, 256)
        EPS = 1e-06
        key = jax.random.key(seed)
        ks = jax.random.split(key, 5)
        return {'emb': jax.random.normal(ks[0], (B, T, E), dtype=jnp.float32), 'latent': jax.random.normal(ks[1], (B, M, L), dtype=jnp.float32), 'Wq': jax.random.normal(ks[2], (E, E), dtype=jnp.float32) * (1.0 / np.sqrt(E)), 'bq': jnp.zeros((E,), dtype=jnp.float32), 'Wk': jax.random.normal(ks[3], (L, E), dtype=jnp.float32) * (1.0 / np.sqrt(L)), 'bk': jnp.zeros((E,), dtype=jnp.float32), 'Wv': jax.random.normal(ks[4], (L, E), dtype=jnp.float32) * (1.0 / np.sqrt(L)), 'bv': jnp.zeros((E,), dtype=jnp.float32), 'gamma': jnp.ones((E,), dtype=jnp.float32), 'beta': jnp.zeros((E,), dtype=jnp.float32)}
    _L0_xattn_all = _L0_xattn_setup()
    _L0_xattn_in = {k: v for k, v in _L0_xattn_all.items() if k in ('Wq', 'bq', 'Wk', 'bk', 'Wv', 'bv', 'gamma', 'beta')}
    del _L0_xattn_all

    def _L1_xattn_setup():
        import jax, jax.numpy as jnp
        import numpy as np
        QUERY_DIM = 512
        KEY_DIM = 256
        HIDDEN_DIM = 512
        B, LQ, LK = (8, 1024, 1024)
        key = jax.random.key(seed)
        ks = jax.random.split(key, 10)
        s_q = 1.0 / np.sqrt(QUERY_DIM)
        s_k = 1.0 / np.sqrt(KEY_DIM)
        s_h = 1.0 / np.sqrt(HIDDEN_DIM)
        return {'query': jax.random.normal(ks[0], (B, LQ, QUERY_DIM), jnp.float32), 'key': jax.random.normal(ks[1], (B, LK, KEY_DIM), jnp.float32), 'Wq': jax.random.uniform(ks[2], (QUERY_DIM, HIDDEN_DIM), jnp.float32, -s_q, s_q), 'bq': jax.random.uniform(ks[3], (HIDDEN_DIM,), jnp.float32, -s_q, s_q), 'Wk': jax.random.uniform(ks[4], (KEY_DIM, HIDDEN_DIM), jnp.float32, -s_k, s_k), 'bk': jax.random.uniform(ks[5], (HIDDEN_DIM,), jnp.float32, -s_k, s_k), 'Wv': jax.random.uniform(ks[6], (KEY_DIM, HIDDEN_DIM), jnp.float32, -s_k, s_k), 'bv': jax.random.uniform(ks[7], (HIDDEN_DIM,), jnp.float32, -s_k, s_k), 'Wo': jax.random.uniform(ks[8], (HIDDEN_DIM, QUERY_DIM), jnp.float32, -s_h, s_h), 'bo': jax.random.uniform(ks[9], (QUERY_DIM,), jnp.float32, -s_h, s_h)}
    _L1_xattn_all = _L1_xattn_setup()
    _L1_xattn_in = {k: v for k, v in _L1_xattn_all.items() if k in ('Wq', 'bq', 'Wk', 'bk', 'Wv', 'bv', 'Wo', 'bo')}
    del _L1_xattn_all
    return {'x': x, 'ctx_512': ctx_512, 'L0_xattn_Wq': _L0_xattn_in['Wq'], 'L0_xattn_bq': _L0_xattn_in['bq'], 'L0_xattn_Wk': _L0_xattn_in['Wk'], 'L0_xattn_bk': _L0_xattn_in['bk'], 'L0_xattn_Wv': _L0_xattn_in['Wv'], 'L0_xattn_bv': _L0_xattn_in['bv'], 'L0_xattn_gamma': _L0_xattn_in['gamma'], 'L0_xattn_beta': _L0_xattn_in['beta'], 'L1_xattn_Wq': _L1_xattn_in['Wq'], 'L1_xattn_bq': _L1_xattn_in['bq'], 'L1_xattn_Wk': _L1_xattn_in['Wk'], 'L1_xattn_bk': _L1_xattn_in['bk'], 'L1_xattn_Wv': _L1_xattn_in['Wv'], 'L1_xattn_bv': _L1_xattn_in['bv'], 'L1_xattn_Wo': _L1_xattn_in['Wo'], 'L1_xattn_bo': _L1_xattn_in['bo']}

def reference(x, ctx_512, L0_xattn_Wq, L0_xattn_bq, L0_xattn_Wk, L0_xattn_bk, L0_xattn_Wv, L0_xattn_bv, L0_xattn_gamma, L0_xattn_beta, L1_xattn_Wq, L1_xattn_bq, L1_xattn_Wk, L1_xattn_bk, L1_xattn_Wv, L1_xattn_bv, L1_xattn_Wo, L1_xattn_bo):
    import jax
    import jax.numpy as jnp

    def _L0_xattn_ref(emb, latent, Wq, bq, Wk, bk, Wv, bv, gamma, beta):
        import jax, jax.numpy as jnp
        import numpy as np
        B, T, E = (8, 2048, 512)
        M, L = (128, 256)
        EPS = 1e-06
        q = jnp.einsum('bte,ef->btf', emb, Wq) + bq
        k = jnp.einsum('bml,le->bme', latent, Wk) + bk
        v = jnp.einsum('bml,le->bme', latent, Wv) + bv
        scale = 1.0 / jnp.sqrt(jnp.asarray(E, dtype=q.dtype))
        w = jnp.einsum('bte,bme->btm', q, k) * scale
        w = jax.nn.softmax(w, axis=1)
        pred = jnp.einsum('btm,bme->bte', w, v)
        x = pred + emb
        mu = jnp.mean(x, axis=-1, keepdims=True)
        var = jnp.var(x, axis=-1, keepdims=True)
        return (x - mu) * jax.lax.rsqrt(var + EPS) * gamma + beta

    def _L1_xattn_ref(query, key, Wq, bq, Wk, bk, Wv, bv, Wo, bo):
        import jax, jax.numpy as jnp
        import numpy as np
        QUERY_DIM = 512
        KEY_DIM = 256
        HIDDEN_DIM = 512
        B, LQ, LK = (8, 1024, 1024)
        scale = HIDDEN_DIM ** (-0.5)
        Q = jnp.einsum('bqd,dh->bqh', query, Wq) + bq
        K = jnp.einsum('bkd,dh->bkh', key, Wk) + bk
        V = jnp.einsum('bkd,dh->bkh', key, Wv) + bv
        scores = jnp.einsum('bqh,bkh->bqk', Q, K) * scale
        weights = jax.nn.softmax(scores, axis=-1)
        attended = jnp.einsum('bqk,bkh->bqh', weights, V)
        out = jnp.einsum('bqh,hd->bqd', attended, Wo) + bo
        return query + out
    x = _L0_xattn_ref(x, ctx_512, L0_xattn_Wq, L0_xattn_bq, L0_xattn_Wk, L0_xattn_bk, L0_xattn_Wv, L0_xattn_bv, L0_xattn_gamma, L0_xattn_beta)
    x = _L1_xattn_ref(x, ctx_512, L1_xattn_Wq, L1_xattn_bq, L1_xattn_Wk, L1_xattn_bk, L1_xattn_Wv, L1_xattn_bv, L1_xattn_Wo, L1_xattn_bo)
    return x

_drawn_inputs = setup_inputs


def setup_inputs(seed=0):
    import zlib

    import numpy as np

    out = dict(_drawn_inputs(seed))
    spreads = {'L0_xattn_bq': (0.0, 0.8),
     'L0_xattn_bk': (0.0, 0.1),
     'L0_xattn_bv': (0.0, 0.1),
     'L0_xattn_gamma': (1.0, 0.2),
     'L0_xattn_beta': (0.0, 0.1)}
    factors = {'L1_xattn_Wq': 2.779,
     'L1_xattn_bq': 8.0,
     'L1_xattn_Wk': 2.768,
     'L1_xattn_bk': 8.0,
     'L1_xattn_bv': 3.01}
    for name, (base, spread) in spreads.items():
        noise = np.random.default_rng([zlib.crc32(name.encode()), seed]).standard_normal(out[name].shape)
        drawn = base * np.exp(spread * noise) if base else spread * noise
        out[name] = jnp.asarray(drawn.astype(out[name].dtype))
    for name, factor in factors.items():
        out[name] = (out[name] * factor).astype(out[name].dtype)
    return out
```

```python
from contextlib import ExitStack

import concourse.bass as bass
from concourse import mybir

F32 = mybir.dt.float32
F32R = mybir.dt.float32r
ALU = mybir.AluOpType
ACT = mybir.ActivationFunctionType
AX_X = mybir.AxisListType.X
P = 128
BANKS = 8
LOWEST = -3.4028235e38
EPS = 1e-6

FRONT = {"xT", "cT", "rb", "y", "s0", "rs", "wc", "pr"}


def tiles(name, n):
    return [(name, k) for k in range(n)]


STEADY = (tiles("xT", 4) + tiles("cT", 2) + tiles("y", 2) + tiles("nT", 4) + tiles("rb", 1) + tiles("s0", 2)
          + tiles("y1", 2) + tiles("wc", 2) + tiles("rs", 1) + tiles("s1", 2) + tiles("pr", 3) + tiles("pt", 2)
          + [("pr", 3)] + tiles("pc", 2) + tiles("out", 4))
PREP0 = tiles("wqT0", 4) + tiles("wkT0", 2) + tiles("wqk0", 2) + tiles("u0", 1) + tiles("c0", 1)
PREP1A = tiles("q1b", 1) + tiles("wqT1", 4) + tiles("wkT1", 2) + tiles("wvT1", 2)
PREP1B = tiles("wqk1", 2) + tiles("u1", 1) + tiles("c1", 1)
PREP1C = tiles("wvo", 2) + tiles("bo1", 1)


def place_banks():
    bank, turn = {}, 0
    for t in STEADY:
        if t[0] in ("rb", "rs"):
            bank[t] = (turn + 3) % BANKS
        else:
            bank[t] = turn % BANKS
            turn += 1
    for n, t in enumerate(PREP0 + PREP1A + PREP1B + PREP1C):
        bank[t] = n % BANKS
    return bank


BANK = place_banks()


def front_only(order):
    return [t for t in order if t[0] in FRONT]


def insert_after(order, tile, extra):
    at = order.index(tile) + 1
    return order[:at] + extra + order[at:]


FIRST = insert_after(insert_after(insert_after(front_only(STEADY), ("y", 1), PREP1A), ("s0", 1), PREP1B),
                     ("wc", 1), PREP1C)
FIRST = PREP0 + FIRST
LAST = [t for t in STEADY if t[0] not in FRONT]


class Iteration:

    def __init__(self, pairs, known, j=None):
        self.pairs, self.known, self.j = pairs, known, j
        self.front = j is not None or known < pairs
        self.back = j is not None or known > 0
        self.parity = known % 2

    def times(self, per, plus):
        return self.known * per + plus if self.j is None else self.j * (2 * per) + (self.known * per + plus)

    def loads(self):
        n = 16 * (self.known // 2 + 1)
        return n if self.j is None else self.j * 16 + n

    def fill(self, tile):
        b = BANK[tile]

        def upto(order, end):
            return sum(1 for t in order[:end] if BANK[t] == b)

        if self.j is None and self.known == 0:
            return upto(FIRST, FIRST.index(tile) + 1)
        order = LAST if self.j is None and self.known == self.pairs else STEADY
        steady = upto(STEADY, len(STEADY))
        return self.times(steady, upto(FIRST, len(FIRST)) - steady + upto(order, order.index(tile) + 1))


def two_cross_attentions(nc, x, ctx, wq0, bq0, wk0, bk0, wv0, bv0, gamma, beta,
                         wq1, bq1, wk1, bk1, wv1, bv1, wo1, bo1, out):
    S, T, D = x.shape
    M, C = ctx.shape[1:]
    PAIRS = S // 2
    KD, KC = D // P, C // P
    J = 2 * T // P
    RT, RM = T // P, M // P
    SCALE = float(D) ** -0.5
    assert (T, M, D, C) == (256, 256, 512, 256) and wq0.shape == (D, D)

    x_rows = x.rearrange("s t d -> (s t) d")
    ctx_rows = ctx.rearrange("s m c -> (s m) c")
    out_rows = out.rearrange("s t d -> (s t) d")

    with ExitStack() as whole:
        def sb(name, shape, dt=F32, scope=whole):
            return scope.enter_context(nc.sbuf_tensor(name, shape, dt))

        def pair(name, shape, scope=whole):
            return sb(name + "_hi", shape, F32R, scope), sb(name + "_lo", shape, F32R, scope)

        def sem(name):
            return whole.enter_context(nc.semaphore(name))

        psum = [whole.enter_context(nc.psum_tensor(f"bank{b}", [P, 512], F32)) for b in range(BANKS)]

        ident = sb("ident", [P, P])
        ones_r = sb("ones_r", [P, P], F32R)
        WQK = [pair("wqk0", [P, KD, C]), pair("wqk1", [P, KD, C])]
        WV0 = pair("wv0", [P, KC, D])
        WVO = pair("wvo", [P, KC, D])
        u_b = [sb("u0_b", [P, D]), sb("u1_b", [P, D])]
        ccol = [sb("c0", [P, KC + 1]), sb("c1", [P, KC + 1])]
        bv0_rows = sb("bv0_rows", [P, D], F32R)
        gamma_b = sb("gamma_b", [P, D])
        beta_b = sb("beta_b", [P, D])
        col = sb("col", [P, 7, KD])
        BQ0, BK0, GAMMA, BETA, BQ1, BK1, BV1 = range(7)
        q1b = sb("q1b", [P, KD])

        XN = [sb("x_even", [P, J, D]), sb("x_odd", [P, J, D])]
        ctxn = sb("ctxn", [P, J, C])
        XT = pair("xT", [P, KD, J * P])
        Y = pair("y", [P, KC, J * P])
        E0 = sb("e0", [P, 2, RM, T])
        N = sb("n", [P, J, D])
        RS = sb("rs", [P, J * P], F32R)
        prod = [sb("prod0", [P, D]), sb("prod1", [P, D])]
        r0 = sb("r0", [P, J])
        r0s = sb("r0s", [P, J])
        RB = sb("rb", [P, J * P])
        mx0, neg0, sum0, rinv0 = (sb(n, [P, J]) for n in ("mx0", "neg0", "sum0", "rinv0"))
        r1, mx1, top1, neg1, sum1, rinv1 = (sb(n, [P, J]) for n in ("r1", "mx1", "top1", "neg1", "sum1", "rinv1"))
        stats = sb("stats", [P, J, 6])
        mv = sb("mv", [P, J, 2])
        var_eps = sb("var_eps", [P, J])
        rstd = sb("rstd", [P, J])
        waited = sb("waited", [P, 2])
        minus_half = sb("minus_half", [P, J])
        CT_even, CN_even = pair("cT_even", [P, KC, J * P]), pair("cn_even", [P, J, C])

        with ExitStack() as stage0:
            wq0_sb = sb("wq0_sb", [P, KD, D], scope=stage0)
            wk0_sb = sb("wk0_sb", [P, KC, D], scope=stage0)
            wv0_sb = sb("wv0_sb", [P, KC, D], scope=stage0)
            wqT0 = sb("wqT0", [P, KD, D], scope=stage0)
            wkT0 = sb("wkT0", [P, KD, C], scope=stage0)
            bv0_b = sb("bv0_b", [P, D], scope=stage0)
            bv0_hi = sb("bv0_hi", [P, D], F32R, scope=stage0)
        CT_odd, CN_odd = pair("cT_odd", [P, KC, J * P]), pair("cn_odd", [P, J, C])
        W = pair("w", [P, 2, RM, T])
        WC = pair("wc", [P, 2, KC, T])
        CT, CN = [CT_even, CT_odd], [CN_even, CN_odd]
        with ExitStack() as stage1:
            wq1_sb = sb("wq1_sb", [P, KD, D], scope=stage1)
            wq1g = sb("wq1g", [P, KD, D], scope=stage1)
            wqT1 = sb("wqT1", [P, KD, D], scope=stage1)
            wk1_sb = sb("wk1_sb", [P, KC, D], scope=stage1)
            wkT1 = sb("wkT1", [P, KD, C], scope=stage1)
            wv1_sb = sb("wv1_sb", [P, KC, D], scope=stage1)
            wvT1 = sb("wvT1", [P, KD, C], scope=stage1)
            wo1_sb = sb("wo1_sb", [P, KD, D], scope=stage1)
            bo1_b = sb("bo1_b", [P, D], scope=stage1)
        NT = pair("nT", [P, KD, J * P])
        Y1 = pair("y1", [P, KC, J * P])
        PT = pair("pt", [P, 2, RM, T])
        PC = pair("pc", [P, 2, KC, T])
        E1 = sb("e1", [P, 2, RT, M])
        R = sb("r", [P, J, D])

        filled = [sem(f"filled{b}") for b in range(BANKS)]
        emptied = [sem(f"emptied{b}") for b in range(BANKS)]
        x_loaded = [sem("x_even_loaded"), sem("x_odd_loaded")]
        ctx_loaded = sem("ctx_loaded")
        ROWS = 4
        rows_in_or_stored = sem("rows_in_or_stored")
        loaded = {n: sem(f"{n}_loaded") for n in
                  ("wq0", "wk0", "wv0", "cols", "wq1", "wk1", "wv1", "wo1")}
        ident_ready, consts_ready, zeroed = sem("ident_ready"), sem("consts_ready"), sem("zeroed")
        wv0_hi, wv0_ready, gamma_scaled = sem("wv0_rounded"), sem("wv0_ready"), sem("gamma_scaled")
        q1b_ready, beta_mid, beta_ready = sem("q1b_ready"), sem("beta_mid"), sem("beta_ready")
        prep_hi = sem("prep_hi")
        hi = {n: sem(f"{n}_hi_ready") for n in ("xT", "cT", "cn", "y", "w", "wc", "nT", "y1", "pt", "pc")}
        cn_lo, w_lo = sem("cn_lo_ready"), sem("w_lo_ready")
        r0_ready, r0s_ready, exp0_ready = sem("r0_ready"), sem("r0s_ready"), sem("exp0_ready")
        mx0_ready, neg0_ready, rinv0_ready = sem("mx0_ready"), sem("neg0_ready"), sem("rinv0_ready")
        bv0_rounded, bv0_zeroed, bv0_ready = sem("bv0_rounded"), sem("bv0_zeroed"), sem("bv0_ready")
        rs_hi_ready = sem("rs_hi_ready")
        stats_ready, mv_ready = sem("stats_ready"), sem("mv_ready")
        var_ready, rstd_ready, n_ready = sem("var_ready"), sem("rstd_ready"), sem("n_ready")
        prod_ready, r1_ready = sem("prod_ready"), sem("r1_ready")
        mx1_ready, top1_ready, neg1_ready, rinv1_ready = (sem("mx1_ready"), sem("top1_ready"),
                                                          sem("neg1_ready"), sem("rinv1_ready"))
        scaled_ready, resid_ready = sem("scaled_ready"), sem("resid_ready")

        block = whole.enter_context(nc.Block())

        def at(tile):
            return psum[BANK[tile]]

        def wait_filled(eng, it, name, k=0):
            eng.wait_ge(filled[BANK[name, k]], it.fill((name, k)))

        def wait_emptied(eng, it, name, k=0):
            eng.wait_ge(emptied[BANK[name, k]], it.fill((name, k)))

        def run(eng, iteration):
            iteration(Iteration(PAIRS, 0))
            with eng.Fori(0, (PAIRS - 2) // 2) as j:
                iteration(Iteration(PAIRS, 1, j))
                iteration(Iteration(PAIRS, 2, j))
            iteration(Iteration(PAIRS, PAIRS - 1))
            iteration(Iteration(PAIRS, PAIRS))

        @block.sync
        def _(sp):
            def known_early(it, value):
                if it.j is not None:
                    sp.compute_val(value)
                return value

            def rows_of(t, start):
                return t[bass.ds(start, J * P), :].rearrange("(j p) d -> p j d", p=P)

            def by_partition(v):
                return v.rearrange("(k p) -> p k", p=P)

            sp.dma_start(wq0_sb[:], wq0.rearrange("(k p) e -> p k e", p=P)).then_inc(loaded["wq0"], 16)
            sp.dma_start(wk0_sb[:], wk0.rearrange("(k p) e -> p k e", p=P)).then_inc(loaded["wk0"], 16)
            with nc.allow_non_contiguous_dma("a few bias vectors, one element per partition"):
                for n, v in enumerate((bq0, bk0, gamma, beta, bq1, bk1, bv1)):
                    sp.dma_start(col[:, n, :], by_partition(v)).then_inc(loaded["cols"], 16)
            sp.dma_start(XN[0][:], rows_of(x_rows, 0)).then_inc(x_loaded[0], 16)
            sp.dma_start(ctxn[:], rows_of(ctx_rows, 0)).then_inc(ctx_loaded, 16)
            sp.dma_start(wv0_sb[:], wv0.rearrange("(k p) e -> p k e", p=P)).then_inc(loaded["wv0"], 16)
            for t, v in ((bv0_b, bv0), (gamma_b, gamma), (beta_b, beta), (bo1_b, bo1)):
                sp.dma_start(t[:], v.partition_broadcast(P)).then_inc(rows_in_or_stored, 16)
            sp.dma_start(wq1_sb[:], wq1.rearrange("(k p) e -> p k e", p=P)).then_inc(loaded["wq1"], 16)
            sp.dma_start(wk1_sb[:], wk1.rearrange("(k p) e -> p k e", p=P)).then_inc(loaded["wk1"], 16)
            sp.dma_start(wv1_sb[:], wv1.rearrange("(k p) e -> p k e", p=P)).then_inc(loaded["wv1"], 16)
            sp.dma_start(wo1_sb[:], wo1.rearrange("(k p) e -> p k e", p=P)).then_inc(loaded["wo1"], 16)

            def iteration(it):
                more = it.j is not None or it.known < PAIRS - 1
                if more:
                    upcoming = known_early(it, it.times(J * P, J * P))
                    cT_filled = known_early(it, it.fill(("cT", KC - 1)))
                    cn_cut = known_early(it, it.times(1, 1))
                if it.back:
                    finished = known_early(it, it.times(J * P, -J * P))
                    n_made = known_early(it, it.times(J, 0))
                    out_made = [known_early(it, it.fill(("out", j))) for j in range(J)]
                if more:
                    if it.back:
                        sp.wait_ge(n_ready, n_made)
                    sp.dma_start(XN[1 - it.parity][:], rows_of(x_rows, upcoming))\
                        .then_inc(x_loaded[1 - it.parity], 16)
                    sp.wait_ge(filled[BANK["cT", KC - 1]], cT_filled)
                    sp.wait_ge(cn_lo, cn_cut)
                    sp.dma_start(ctxn[:], rows_of(ctx_rows, upcoming)).then_inc(ctx_loaded, 16)
                if it.back:
                    for j in range(J):
                        sp.wait_ge(emptied[BANK["out", j]], out_made[j])
                    sp.dma_start(rows_of(out_rows, finished), R[:]).then_inc(rows_in_or_stored, 16)

            run(sp, iteration)
            sp.wait_ge(rows_in_or_stored, 16 * (ROWS + PAIRS))

        @block.tensor
        def _(pe):
            def begin(it, name, k=0):
                n = it.fill((name, k))
                if it.j is not None or n > 1:
                    pe.wait_ge(emptied[BANK[name, k]], n - 1)
                return at((name, k))

            def end(mm, name, k=0):
                mm.then_inc(filled[BANK[name, k]], 1)

            def passes(w, m):
                return ((w[0], m[0]), (w[0], m[1]), (w[1], m[0]))

            def product(dst, terms, last=True, first=True):
                for n, (w, m) in enumerate(terms):
                    mm = pe.matmul(dst, w, m, start=first and n == 0, stop=last and n == len(terms) - 1)
                return mm

            def transposes(it, name, k, blocks):
                dst = begin(it, name, k)
                for n, src in enumerate(blocks):
                    mm = pe.transpose(dst[:, n * P:(n + 1) * P], src, ident[:])
                end(mm, name, k)

            def weight_products(it, L, wqT, wkT):
                bq = col[:, BQ0, :] if L == 0 else q1b[:]
                bk = col[:, BK0 if L == 0 else BK1, :]
                for h in range(KD):
                    wait_emptied(pe, it, f"wqT{L}", h)
                for h in range(KC):
                    wait_emptied(pe, it, f"wkT{L}", h)
                for g in range(KD // 2):
                    dst = begin(it, f"wqk{L}", g)
                    for h in range(2):
                        k = 2 * g + h
                        mm = product(dst[:, h * C:(h + 1) * C],
                                     [(wqT[:, e, k * P:(k + 1) * P], wkT[:, e, :]) for e in range(KD)])
                    end(mm, f"wqk{L}", g)
                dst = begin(it, f"u{L}")
                end(product(dst[:, :D], [(bk[:, e:e + 1].to_broadcast([P, P]), wqT[:, e, :])
                                         for e in range(KD)]), f"u{L}")
                dst = begin(it, f"c{L}")
                for c in range(KC):
                    product(dst[:, c:c + 1], [(wkT[:, e, c * P:(c + 1) * P], bq[:, e:e + 1]) for e in range(KD)])
                end(product(dst[:, KC:KC + 1], [(bk[:, e:e + 1].to_broadcast([P, P]), bq[:, e:e + 1])
                                                for e in range(KD)]), f"c{L}")

            def prepare0(it):
                pe.wait_ge(ident_ready, 2)
                pe.wait_ge(loaded["wq0"], 16)
                for e in range(KD):
                    transposes(it, "wqT0", e, [wq0_sb[:, k, e * P:(e + 1) * P] for k in range(KD)])
                pe.wait_ge(loaded["wk0"], 16)
                for g in range(2):
                    transposes(it, "wkT0", g, [wk0_sb[:, c, e * P:(e + 1) * P]
                                               for e in (2 * g, 2 * g + 1) for c in range(KC)])
                pe.wait_ge(loaded["cols"], 16 * 7)
                weight_products(it, 0, wqT0, wkT0)

            def prepare1a(it):
                pe.wait_ge(loaded["wq1"], 16)
                dst = begin(it, "q1b")
                for h in range(KD):
                    mm = product(dst[:, h:h + 1], [(wq1_sb[:, k, h * P:(h + 1) * P], col[:, BETA, k:k + 1])
                                                   for k in range(KD)])
                end(mm, "q1b")
                pe.wait_ge(gamma_scaled, KD)
                for e in range(KD):
                    transposes(it, "wqT1", e, [wq1g[:, k, e * P:(e + 1) * P] for k in range(KD)])
                for name, t, arrived in (("wkT1", wk1_sb, "wk1"), ("wvT1", wv1_sb, "wv1")):
                    pe.wait_ge(loaded[arrived], 16)
                    for g in range(2):
                        transposes(it, name, g, [t[:, c, e * P:(e + 1) * P]
                                                 for e in (2 * g, 2 * g + 1) for c in range(KC)])

            def prepare1b(it):
                wait_emptied(pe, it, "q1b")
                weight_products(it, 1, wqT1, wkT1)

            def prepare1c(it):
                for g in range(2):
                    wait_emptied(pe, it, "wvT1", g)
                pe.wait_ge(loaded["wo1"], 16)
                for c in range(KC):
                    dst = begin(it, "wvo", c)
                    end(product(dst[:, :D], [(wvT1[:, h, c * P:(c + 1) * P], wo1_sb[:, h, :])
                                             for h in range(KD)]), "wvo", c)
                dst = begin(it, "bo1")
                end(product(dst[:, :D], [(col[:, BV1, h:h + 1].to_broadcast([P, P]), wo1_sb[:, h, :])
                                         for h in range(KD)]), "bo1")

            def transpose_inputs(it):
                xn = XN[it.parity]
                pe.wait_ge(x_loaded[it.parity], it.loads())
                for k in range(KD):
                    transposes(it, "xT", k, [xn[:, j, k * P:(k + 1) * P] for j in range(J)])
                pe.wait_ge(ctx_loaded, it.times(16, 16))
                for c in range(KC):
                    transposes(it, "cT", c, [ctxn[:, j, c * P:(c + 1) * P] for j in range(J)])

            def transpose_n(it):
                pe.wait_ge(n_ready, it.times(J, 0))
                for k in range(KD):
                    transposes(it, "nT", k, [N[:, j, k * P:(k + 1) * P] for j in range(J)])

            def project(it, name, source, wqk, src):
                dst = [begin(it, name, c) for c in range(KC)]
                for k in range(KD):
                    wait_emptied(pe, it, source, k)
                    for c in range(KC):
                        w = [h[:, k, c * P:(c + 1) * P] for h in wqk]
                        mm = product(dst[c][:], passes(w, [h[:, k, :] for h in src]),
                                     first=k == 0, last=k == KD - 1)
                        if k == KD - 1:
                            end(mm, name, c)

            def spread_r0(it):
                pe.wait_ge(r0s_ready, it.times(1, 1))
                transposes(it, "rb", 0, [r0s[:, j:j + 1].to_broadcast([P, P]) for j in range(J)])

            def scores0(it):
                ct = CT[it.parity]
                for c in range(KC):
                    wait_emptied(pe, it, "y", c)
                for c in range(KC):
                    wait_emptied(pe, it, "cT", c)
                for b in range(2):
                    dst = begin(it, "s0", b)
                    for mt in range(RM):
                        m0 = b * M + mt * P
                        part = dst[:, mt * T:(mt + 1) * T]
                        terms = []
                        for c in range(KC):
                            terms += passes([h[:, c, m0:m0 + P] for h in ct],
                                            [h[:, c, b * T:(b + 1) * T] for h in Y])
                        mm = product(part, terms)
                    end(mm, "s0", b)

            def scores1(it):
                ct = CT[1 - it.parity]
                for c in range(KC):
                    wait_emptied(pe, it, "y1", c)
                for b in range(2):
                    dst = begin(it, "s1", b)
                    for tt in range(RT):
                        t0 = b * T + tt * P
                        terms = []
                        for c in range(KC):
                            terms += passes([h[:, c, t0:t0 + P] for h in Y1],
                                            [h[:, c, b * M:(b + 1) * M] for h in ct])
                        mm = product(dst[:, tt * M:(tt + 1) * M], terms)
                    end(mm, "s1", b)

            def weigh(it, name, b, cn, probs):
                dst = begin(it, name, b)
                for ct in range(KC):
                    terms = []
                    for mt in range(RM):
                        terms += passes([h[:, b * RM + mt, ct * P:(ct + 1) * P] for h in cn],
                                        [h[:, b, mt, :] for h in probs])
                    mm = product(dst[:, ct * T:(ct + 1) * T], terms)
                end(mm, name, b)

            def weigh0(it, b):
                pe.wait_ge(w_lo, it.times(2 * RM, (b + 1) * RM))
                if b == 0:
                    pe.wait_ge(cn_lo, it.times(1, 1))
                weigh(it, "wc", b, CN[it.parity], W)

            def row_sums(it):
                dst = begin(it, "rs")
                end(product(dst[:], [(ones_r[:], h[:, :, mt, :]) for mt in range(RM) for h in W]), "rs")

            def transpose_probs(it, b):
                wait_emptied(pe, it, "s1", b)
                transposes(it, "pt", b, [E1[:, b, tt, mt * P:(mt + 1) * P] for mt in range(RM) for tt in range(RT)])

            def apply(it, name, source, j, left, right):
                b, tt = divmod(j, RT)
                if tt == 0:
                    wait_emptied(pe, it, source, b)
                dst = begin(it, name, j)
                terms = []
                for ct in range(KC):
                    terms += passes([h[:, b, ct, tt * P:(tt + 1) * P] for h in left], [h[:, ct, :] for h in right])
                if name == "pr":
                    if j == 0:
                        wait_emptied(pe, it, "rs")
                    terms.append((RS[:, j * P:(j + 1) * P], bv0_rows[:]))
                end(product(dst[:], terms), name, j)

            def iteration(it):
                begin_it = it.j is None and it.known == 0
                if begin_it:
                    prepare0(it)
                if it.front:
                    transpose_inputs(it)
                    project(it, "y", "xT", WQK[0], XT)
                if begin_it:
                    prepare1a(it)
                if it.back:
                    transpose_n(it)
                if it.front:
                    spread_r0(it)
                    scores0(it)
                if begin_it:
                    prepare1b(it)
                if it.back:
                    project(it, "y1", "nT", WQK[1], NT)
                if it.front:
                    weigh0(it, 0)
                    weigh0(it, 1)
                    row_sums(it)
                if begin_it:
                    prepare1c(it)
                if it.back:
                    scores1(it)
                if it.front:
                    if begin_it:
                        pe.wait_ge(wv0_ready, 1)
                        pe.wait_ge(bv0_ready, 3)
                    for j in range(J - 1):
                        apply(it, "pr", "wc", j, WC, WV0)
                if it.back:
                    transpose_probs(it, 0)
                    transpose_probs(it, 1)
                if it.front:
                    apply(it, "pr", "wc", J - 1, WC, WV0)
                if it.back:
                    for b in range(2):
                        wait_emptied(pe, it, "pt", b)
                        weigh(it, "pc", b, CN[1 - it.parity], PT)
                    for j in range(J):
                        apply(it, "out", "pc", j, PC, WVO)

            pe.wait_ge(consts_ready, 2)
            run(pe, iteration)

        @block.scalar
        def _(act):
            def round_bank(it, name, k, dst, bias=None, scale=None):
                wait_filled(act, it, name, k)
                if bias is not None:
                    i = act.activation(dst, at((name, k))[:], ACT.Identity, bias=bias)
                elif scale is not None:
                    i = act.activation(dst, at((name, k))[:], ACT.Copy, scale=scale)
                else:
                    i = act.activation(dst, at((name, k))[:], ACT.Copy)
                i.then_inc(hi[name] if name in hi else prep_hi, 1)

            def prep_copy(it, name, k, dst, scale=1.0):
                wait_filled(act, it, name, k)
                src = at((name, k))[:, 0:dst.free_size()] if len(dst.shape) == 2 else at((name, k))[:]
                act.activation(dst, src, ACT.Copy, scale=scale).then_inc(emptied[BANK[name, k]], 1)

            def two(t, g):
                return t[:, 2 * g:2 * g + 2, :].rearrange("p k c -> p (k c)")

            def prepare0(it):
                for e in range(KD):
                    prep_copy(it, "wqT0", e, wqT0[:, e, :])
                for g in range(2):
                    prep_copy(it, "wkT0", g, two(wkT0, g))
                act.wait_ge(loaded["wv0"], 16)
                act.activation(WV0[0][:], wv0_sb[:], ACT.Copy).then_inc(wv0_hi, 1)
                act.wait_ge(rows_in_or_stored, 16 * ROWS)
                act.activation(bv0_hi[:], bv0_b[:], ACT.Copy).then_inc(bv0_rounded, 1)
                act.wait_ge(bv0_rounded, 1)
                act.wait_ge(bv0_zeroed, 1)
                for row in (0, 32):
                    act.activation(bv0_rows[row:row + 1, :], bv0_hi[row:row + 1, :].bitcast(F32), ACT.Copy)\
                       .then_inc(bv0_ready, 1)
                for g in range(KD // 2):
                    round_bank(it, "wqk0", g, two(WQK[0][0], g), scale=SCALE)
                prep_copy(it, "u0", 0, u_b[0][:], SCALE)
                prep_copy(it, "c0", 0, ccol[0][:], SCALE)

            def prepare1a(it):
                act.wait_ge(loaded["cols"], 16 * 7)
                act.wait_ge(loaded["wq1"], 16)
                for k in range(KD):
                    act.activation(wq1g[:, k, :], wq1_sb[:, k, :], ACT.Copy,
                                   scale=col[:, GAMMA, k:k + 1]).then_inc(gamma_scaled, 1)
                for e in range(KD):
                    prep_copy(it, "wqT1", e, wqT1[:, e, :])
                for g in range(2):
                    prep_copy(it, "wkT1", g, two(wkT1, g))
                for g in range(2):
                    prep_copy(it, "wvT1", g, two(wvT1, g))

            def prepare1b(it):
                for g in range(KD // 2):
                    round_bank(it, "wqk1", g, two(WQK[1][0], g), scale=SCALE)
                prep_copy(it, "u1", 0, u_b[1][:], SCALE)
                prep_copy(it, "c1", 0, ccol[1][:], SCALE)

            def prepare1c(it):
                for c in range(KC):
                    round_bank(it, "wvo", c, WVO[0][:, c, :])

            def softmax0(it):
                for b in range(2):
                    act.wait_ge(neg0_ready, it.times(2, b + 1))
                    for mt in range(RM):
                        q = b * RM + mt
                        e = act.activation(E0[:, b, mt, :], E0[:, b, mt, :], ACT.Exp,
                                           bias=neg0[:, q:q + 1], accum_out=sum0[:, q:q + 1])
                    e.then_inc(exp0_ready, 1)
                for b in range(2):
                    act.wait_ge(rinv0_ready, it.times(2, b + 1))
                    for mt in range(RM):
                        q = b * RM + mt
                        act.activation(W[0][:, b, mt, :], E0[:, b, mt, :], ACT.Copy,
                                       scale=rinv0[:, q:q + 1]).then_inc(hi["w"], 1)

            def softmax1(it):
                for b in range(2):
                    act.wait_ge(neg1_ready, it.times(2, b - 1))
                    for tt in range(RT):
                        q = b * RT + tt
                        e = act.activation(E1[:, b, tt, :], at(("s1", b))[:, tt * M:(tt + 1) * M], ACT.Exp,
                                           bias=neg1[:, q:q + 1], accum_out=sum1[:, q:q + 1])
                    e.then_inc(emptied[BANK["s1", b]], 1)

            def row_terms(it):
                for j in range(J):
                    act.wait_ge(prod_ready, it.times(J, j + 1 - J))
                    act.activation(prod[j % 2][:], prod[j % 2][:], ACT.Copy,
                                   accum_out=r1[:, j:j + 1]).then_inc(r1_ready, 1)

            def halves(t, b):
                return t[:, b].rearrange("p k t -> p (k t)")

            def iteration(it):
                begin_it = it.j is None and it.known == 0
                if begin_it:
                    prepare0(it)
                if it.front:
                    for k in range(KD):
                        round_bank(it, "xT", k, XT[0][:, k, :])
                    for c in range(KC):
                        round_bank(it, "cT", c, CT[it.parity][0][:, c, :])
                    act.wait_ge(ctx_loaded, it.times(16, 16))
                    act.activation(CN[it.parity][0][:], ctxn[:], ACT.Copy).then_inc(hi["cn"], 1)
                    for c in range(KC):
                        round_bank(it, "y", c, Y[0][:, c, :], bias=ccol[0][:, c:c + 1])
                if begin_it:
                    prepare1a(it)
                if it.back:
                    for k in range(KD):
                        round_bank(it, "nT", k, NT[0][:, k, :])
                if it.front:
                    prep_copy(it, "rb", 0, RB[:])
                    softmax0(it)
                if begin_it:
                    prepare1b(it)
                if it.back:
                    row_terms(it)
                    for c in range(KC):
                        round_bank(it, "y1", c, Y1[0][:, c, :], bias=ccol[1][:, c:c + 1])
                if it.front:
                    for b in range(2):
                        round_bank(it, "wc", b, halves(WC[0], b))
                    wait_filled(act, it, "rs")
                    act.activation(RS[:], at(("rs", 0))[:], ACT.Copy).then_inc(rs_hi_ready, 1)
                if begin_it:
                    prepare1c(it)
                if it.back:
                    softmax1(it)
                    for b in range(2):
                        round_bank(it, "pt", b, halves(PT[0], b))
                    for b in range(2):
                        round_bank(it, "pc", b, halves(PC[0], b))

            run(act, iteration)

        @block.vector
        def _(dve):
            rounded = {"prep": 0}

            def low(it, name, k, dst, high, bias=None, scale=None, per=0, back=0):
                dve.wait_ge(hi[name], it.times(per, k + 1 - back * per))
                src = at((name, k))[:]
                if bias is not None:
                    i = dve.scalar_tensor_tensor(dst, src, bias, high.bitcast(F32), ALU.add, ALU.subtract)
                else:
                    i = dve.tensor_tensor(dst, src, high.bitcast(F32), ALU.subtract)
                i.then_inc(emptied[BANK[name, k]], 1)

            def prep_low(it, name, k, dst, high, scale):
                rounded["prep"] += 1
                dve.wait_ge(prep_hi, rounded["prep"])
                dve.scalar_tensor_tensor(dst, at((name, k))[:], scale, high.bitcast(F32), ALU.mult,
                                         ALU.subtract).then_inc(emptied[BANK[name, k]], 1)

            def two(t, g):
                return t[:, 2 * g:2 * g + 2, :].rearrange("p k c -> p (k c)")

            def prepare0(it):
                dve.wait_ge(bv0_rounded, 1)
                dve.wait_ge(bv0_zeroed, 1)
                row = slice(64, 65)
                dve.tensor_tensor(bv0_rows[row, :], bv0_b[row, :], bv0_hi[row, :].bitcast(F32), ALU.subtract)\
                   .then_inc(bv0_ready, 1)
                dve.wait_ge(wv0_hi, 1)
                dve.tensor_tensor(WV0[1][:], wv0_sb[:], WV0[0][:].bitcast(F32), ALU.subtract).then_inc(wv0_ready, 1)
                for g in range(KD // 2):
                    prep_low(it, "wqk0", g, two(WQK[0][1], g), two(WQK[0][0], g), SCALE)

            def prepare1a(it):
                wait_filled(dve, it, "q1b")
                dve.wait_ge(loaded["cols"], 16 * 7)
                dve.tensor_tensor(q1b[:], at(("q1b", 0))[:, 0:KD], col[:, BQ1, :], ALU.add)\
                   .then_inc(emptied[BANK["q1b", 0]], 1)

            def prepare1b(it):
                for g in range(KD // 2):
                    prep_low(it, "wqk1", g, two(WQK[1][1], g), two(WQK[1][0], g), SCALE)

            def prepare1c(it):
                for c in range(KC):
                    prep_low(it, "wvo", c, WVO[1][:, c, :], WVO[0][:, c, :], 1.0)
                wait_filled(dve, it, "bo1")
                dve.wait_ge(rows_in_or_stored, 16 * ROWS)
                dve.tensor_tensor(bo1_b[:], at(("bo1", 0))[:, 0:D], bo1_b[:], ALU.add)\
                   .then_inc(emptied[BANK["bo1", 0]], 1)
                wait_emptied(dve, it, "bo1")
                dve.tensor_tensor(beta_b[:], beta_b[:], bo1_b[:], ALU.add).then_inc(beta_ready, 1)

            def row_terms0(it):
                dve.wait_ge(x_loaded[it.parity], it.loads())
                if it.j is None and it.known == 0:
                    wait_emptied(dve, it, "u0")
                    wait_emptied(dve, it, "c0")
                for j in range(J):
                    if it.j is not None or it.known or j:
                        dve.wait_ge(r0_ready, it.times(J, j))
                    dve.tensor_tensor_reduce(RB[:], XN[it.parity][:, j, :], u_b[0][:], 1.0, 0.0, ALU.mult,
                                             ALU.add, r0[:, j:j + 1]).then_inc(r0_ready, 1)
                dve.wait_ge(r0_ready, it.times(J, J))
                dve.tensor_scalar(r0s[:], r0[:], ccol[0][:, KC:KC + 1], None, ALU.add).then_inc(r0s_ready, 1)

            def maxima0(it):
                for b in range(2):
                    if b == 0:
                        wait_emptied(dve, it, "rb")
                    wait_filled(dve, it, "s0", b)
                    dve.memset(waited[:, b:b + 1], 0.0)
                    for mt in range(RM):
                        q = b * RM + mt
                        i = dve.tensor_tensor_reduce(E0[:, b, mt, :], at(("s0", b))[:, mt * T:(mt + 1) * T],
                                                     RB[:, b * T:(b + 1) * T], 1.0, LOWEST, ALU.add, ALU.max,
                                                     mx0[:, q:q + 1])
                        i.then_inc(*((emptied[BANK["s0", b]], 1) if mt == RM - 1 else (mx0_ready, 1)))
                    dve.wait_ge(mx0_ready, it.times(2, b + 1))
                    wait_emptied(dve, it, "s0", b)
                    q = slice(b * RM, (b + 1) * RM)
                    dve.tensor_scalar(neg0[:, q], mx0[:, q], -1.0, None, ALU.mult).then_inc(neg0_ready, 1)

            def maxima1(it):
                s = ccol[1][:, KC:KC + 1]
                dve.wait_ge(r1_ready, it.times(J, 0))
                for b in range(2):
                    wait_filled(dve, it, "s1", b)
                    q = slice(b * RT, (b + 1) * RT)
                    dve.tensor_reduce(mx1[:, q], at(("s1", b))[:].rearrange("p (t m) -> p t m", t=RT), AX_X,
                                      ALU.max).then_inc(mx1_ready, 1)
                    dve.wait_ge(mx1_ready, it.times(2, b - 1))
                    dve.scalar_tensor_tensor(top1[:, q], r1[:, q], s, mx1[:, q], ALU.add, ALU.add)\
                       .then_inc(top1_ready, 1)
                    dve.wait_ge(top1_ready, it.times(2, b - 1))
                    dve.scalar_tensor_tensor(neg1[:, q], r1[:, q], s, top1[:, q], ALU.add, ALU.subtract)\
                       .then_inc(neg1_ready, 1)

            def normalise0(it):
                for b in range(2):
                    dve.wait_ge(exp0_ready, it.times(2, b + 1))
                    q = slice(b * RM, (b + 1) * RM)
                    dve.reciprocal(rinv0[:, q], sum0[:, q]).then_inc(rinv0_ready, 1)
                for b in range(2):
                    for mt in range(RM):
                        q = b * RM + mt
                        dve.wait_ge(hi["w"], it.times(2 * RM, q + 1))
                        dve.scalar_tensor_tensor(W[1][:, b, mt, :], E0[:, b, mt, :], rinv0[:, q:q + 1],
                                                 W[0][:, b, mt, :].bitcast(F32), ALU.mult, ALU.subtract)\
                           .then_inc(w_lo, 1)

            def norm_and_output(it):
                xn = XN[it.parity]

                def add(j):
                    wait_filled(dve, it, "pr", j)
                    dve.tensor_tensor(xn[:, j, :], at(("pr", j))[:], xn[:, j, :], ALU.add)\
                       .then_inc(emptied[BANK["pr", j]], 1)

                def statistics(j):
                    wait_emptied(dve, it, "pr", j)
                    dve.bn_stats(stats[:, j, :], xn[:, j, :]).then_inc(stats_ready, 1)

                def aggregate(b):
                    for j in range(b * RT, (b + 1) * RT):
                        dve.bn_aggr(mv[:, j, :], stats[:, j, :]).then_inc(mv_ready, 1)
                    dve.wait_ge(mv_ready, it.times(J, (b + 1) * RT))
                    q = slice(b * RT, (b + 1) * RT)
                    dve.tensor_scalar(var_eps[:, q], mv[:, q, 1], EPS, None, ALU.add).then_inc(var_ready, 1)

                def normalise(j):
                    dve.wait_ge(rstd_ready, it.times(2, j // RT + 1))
                    dve.tensor_scalar(N[:, j, :], xn[:, j, :], mv[:, j, 0:1], rstd[:, j:j + 1], ALU.subtract,
                                      ALU.mult).then_inc(n_ready, 1)

                def output(j):
                    wait_filled(dve, it, "out", j)
                    dve.wait_ge(resid_ready, it.times(J, j + 1 - J))
                    dve.scalar_tensor_tensor(R[:, j, :], at(("out", j))[:], rinv1[:, j:j + 1], R[:, j, :],
                                             ALU.mult, ALU.add).then_inc(emptied[BANK["out", j]], 1)

                def cut_pc(b):
                    low(it, "pc", b, halves(PC[1], b), halves(PC[0], b), per=2, back=1)

                def cut_pt(b):
                    low(it, "pt", b, halves(PT[1], b), halves(PT[0], b), per=2, back=1)

                if it.front:
                    add(0)
                    statistics(0)
                    add(1)
                    statistics(1)
                    dve.wait_ge(stats_ready, it.times(J, RT))
                    add(2)
                    aggregate(0)
                if it.back:
                    cut_pt(0)
                    cut_pt(1)
                    wait_emptied(dve, it, "s1", 1)
                    dve.reciprocal(rinv1[:], sum1[:]).then_inc(rinv1_ready, 1)
                if it.front:
                    add(3)
                    statistics(2)
                if it.back:
                    cut_pc(0)
                if it.front:
                    statistics(3)
                if it.back:
                    cut_pc(1)
                if it.front:
                    if it.back:
                        wait_filled(dve, it, "nT", KD - 1)
                        dve.wait_ge(scaled_ready, it.times(J, 0))
                    normalise(0)
                    dve.wait_ge(stats_ready, it.times(J, J))
                    normalise(1)
                    aggregate(1)
                if it.back:
                    dve.wait_ge(rinv1_ready, it.times(1, 0))
                    output(0)
                if it.front:
                    normalise(2)
                    normalise(3)
                if it.back:
                    for j in range(1, J):
                        output(j)

            def halves(t, b):
                return t[:, b].rearrange("p k t -> p (k t)")

            def iteration(it):
                begin_it = it.j is None and it.known == 0
                if begin_it:
                    prepare0(it)
                if it.front:
                    for k in range(KD):
                        low(it, "xT", k, XT[1][:, k, :], XT[0][:, k, :], per=KD)
                    for c in range(KC):
                        low(it, "cT", c, CT[it.parity][1][:, c, :], CT[it.parity][0][:, c, :], per=KC)
                    row_terms0(it)
                    for c in range(KC):
                        low(it, "y", c, Y[1][:, c, :], Y[0][:, c, :], bias=ccol[0][:, c:c + 1], per=KC)
                if begin_it:
                    prepare1a(it)
                if it.back:
                    for k in range(KD):
                        low(it, "nT", k, NT[1][:, k, :], NT[0][:, k, :], per=KD, back=1)
                if it.front:
                    maxima0(it)
                    normalise0(it)
                if begin_it:
                    prepare1b(it)
                if it.back:
                    for c in range(KC):
                        low(it, "y1", c, Y1[1][:, c, :], Y1[0][:, c, :], bias=ccol[1][:, c:c + 1], per=KC, back=1)
                if it.front:
                    for b in range(2):
                        low(it, "wc", b, halves(WC[1], b), halves(WC[0], b), per=2)
                    dve.wait_ge(rs_hi_ready, it.times(1, 1))
                    q = slice(32, 64)
                    dve.tensor_tensor(RS[q, :], at(("rs", 0))[q, :], RS[q, :].bitcast(F32), ALU.subtract)\
                       .then_inc(emptied[BANK["rs", 0]], 1)
                if begin_it:
                    prepare1c(it)
                if it.back:
                    maxima1(it)
                norm_and_output(it)

            run(dve, iteration)

        @block.gpsimd
        def _(pool):
            pool.memset(ident[:], 0.0).then_inc(ident_ready, 1)
            pool.wait_ge(ident_ready, 1)
            pool.affine_select(out=ident[:], in_=ident[:], compare_op=ALU.not_equal, fill=1.0, base=0,
                               pattern=[[-1, P]], channel_multiplier=1).then_inc(ident_ready, 1)
            pool.memset(ones_r[:].bitcast(F32), 1.0).then_inc(consts_ready, 1)
            pool.memset(bv0_rows[:].bitcast(F32), 0.0).then_inc(bv0_zeroed, 1)
            pool.memset(minus_half[:], -0.5).then_inc(consts_ready, 1)
            pool.wait_ge(consts_ready, 2)

            def cut_ctx(it):
                pool.wait_ge(hi["cn"], it.times(1, 1))
                pool.tensor_tensor(CN[it.parity][1][:], ctxn[:], CN[it.parity][0][:].bitcast(F32), ALU.subtract)\
                    .then_inc(cn_lo, 1)

            def rstds(it):
                for b in range(2):
                    pool.wait_ge(var_ready, it.times(2, b + 1))
                    q = slice(b * RT, (b + 1) * RT)
                    pool.tensor_tensor(rstd[:, q], var_eps[:, q], minus_half[:, q], ALU.pow).then_inc(rstd_ready, 1)

            def row_products(it):
                for j in range(J):
                    pool.wait_ge(n_ready, it.times(J, j + 1 - J))
                    if j >= 2:
                        pool.wait_ge(r1_ready, it.times(J, j - 1 - J))
                    pool.tensor_tensor(prod[j % 2][:], N[:, j, :], u_b[1][:], ALU.mult).then_inc(prod_ready, 1)

            def residual(it):
                pool.wait_ge(rows_in_or_stored, it.times(16, 16 * (ROWS - 1)))
                for j in range(J):
                    pool.tensor_tensor(R[:, j, :], N[:, j, :], gamma_b[:], ALU.mult).then_inc(scaled_ready, 1)
                for j in range(J):
                    pool.wait_ge(scaled_ready, it.times(J, j + 1 - J))
                    pool.tensor_tensor(R[:, j, :], R[:, j, :], beta_b[:], ALU.add).then_inc(resid_ready, 1)

            def iteration(it):
                if it.front:
                    cut_ctx(it)
                if it.back:
                    row_products(it)
                    residual(it)
                if it.front:
                    rstds(it)

            def guarded(it):
                if it.j is None and it.known == 0:
                    iteration(it)
                    wait_emptied(pool, it, "u1")
                    pool.wait_ge(beta_ready, 1)
                else:
                    iteration(it)

            run(pool, guarded)


_INS = ['x', 'ctx_512', 'L0_xattn_Wq', 'L0_xattn_bq', 'L0_xattn_Wk', 'L0_xattn_bk', 'L0_xattn_Wv', 'L0_xattn_bv',
        'L0_xattn_gamma', 'L0_xattn_beta', 'L1_xattn_Wq', 'L1_xattn_bq', 'L1_xattn_Wk', 'L1_xattn_bk',
        'L1_xattn_Wv', 'L1_xattn_bv', 'L1_xattn_Wo', 'L1_xattn_bo']


def kernel(**inputs):
    import numpy as _np
    import concourse.bacc as _bacc
    from concourse import mybir as _mybir
    from concourse.bass_utils import run_bass_kernel_spmd as _run

    nc = _bacc.Bacc("TRN2", target_bir_lowering=False, num_devices=1)
    arrays, args = {}, []
    for name in _INS:
        a = _np.ascontiguousarray(inputs[name])
        arrays[f"in_{name}_dram"] = a
        args.append(nc.dram_tensor(f"in_{name}_dram", a.shape, _mybir.dt.from_np(a.dtype), kind="ExternalInput").ap())
    args.append(nc.dram_tensor("out_0_dram", inputs['x'].shape, _mybir.dt.float32, kind="ExternalOutput").ap())
    two_cross_attentions(nc, *args)
    r = _run(nc, [arrays], core_ids=[0])
    return r.results[0]["out_0_dram"]
```

```python
from contextlib import ExitStack

import concourse.bass as bass
from concourse import mybir

F32 = mybir.dt.float32
F32R = mybir.dt.float32r
ALU = mybir.AluOpType
ACT = mybir.ActivationFunctionType
AX_X = mybir.AxisListType.X
P = 128
BANKS = 8
LOWEST = -3.4028235e38
EPS = 1e-6

FRONT = {"xT", "cT", "rb", "y", "s0", "rs", "wc", "pr"}


def tiles(name, n):
    return [(name, k) for k in range(n)]


STEADY = (tiles("xT", 4) + tiles("cT", 2) + tiles("y", 2) + tiles("nT", 4) + tiles("rb", 1) + tiles("s0", 2)
          + tiles("y1", 2) + tiles("rs", 1) + tiles("wc", 2) + tiles("s1", 2) + tiles("pr", 2) + tiles("pt", 2)
          + [("pr", 2), ("pc", 0), ("pr", 3), ("pc", 1)] + tiles("out", 4))
PREP0 = tiles("wqT0", 4) + tiles("wkT0", 2) + tiles("wqk0", 2) + tiles("u0", 1)
PREP1A = tiles("wqT1", 4) + tiles("wkT1", 2)
PREP1B = tiles("wvT1", 2) + tiles("wqk1", 2) + tiles("q1", 1)
PREP1C = tiles("u1", 1) + tiles("wvo", 2) + tiles("bo1", 1)
PREP_BANKS = (7, 0, 1, 2, 3, 4, 5, 6, 7) + (0, 1, 2, 3, 4, 5) + (6, 7, 2, 3, 4) + (3, 6, 7, 4)


def place_banks():
    bank, turn = {}, 0
    for t in STEADY:
        if t[0] in ("rb", "rs"):
            bank[t] = (turn + (3 if t[0] == "rb" else 5)) % BANKS
        else:
            bank[t] = turn % BANKS
            turn += 1
    bank.update(zip(PREP0 + PREP1A + PREP1B + PREP1C, PREP_BANKS))
    return bank


BANK = place_banks()


def front_only(order):
    return [t for t in order if t[0] in FRONT]


def insert_after(order, tile, extra):
    at = order.index(tile) + 1
    return order[:at] + extra + order[at:]


FIRST = insert_after(insert_after(insert_after(front_only(STEADY), ("y", 1), PREP1A), ("s0", 1), PREP1B),
                     ("pr", 3), PREP1C)
FIRST = PREP0 + FIRST
LAST = [t for t in STEADY if t[0] not in FRONT]


class Iteration:

    def __init__(self, pairs, known, j=None):
        self.pairs, self.known, self.j = pairs, known, j
        self.front = j is not None or known < pairs
        self.back = j is not None or known > 0
        self.parity = known % 2

    def times(self, per, plus):
        return self.known * per + plus if self.j is None else self.j * (2 * per) + (self.known * per + plus)

    def loads(self):
        n = 16 * (self.known // 2 + 1)
        return n if self.j is None else self.j * 16 + n

    def fill(self, tile):
        b = BANK[tile]

        def upto(order, end):
            return sum(1 for t in order[:end] if BANK[t] == b)

        if self.j is None and self.known == 0:
            return upto(FIRST, FIRST.index(tile) + 1)
        order = LAST if self.j is None and self.known == self.pairs else STEADY
        steady = upto(STEADY, len(STEADY))
        return self.times(steady, upto(FIRST, len(FIRST)) - steady + upto(order, order.index(tile) + 1))


def two_cross_attentions(nc, x, ctx, wq0, bq0, wk0, bk0, wv0, bv0, gamma, beta,
                         wq1, bq1, wk1, bk1, wv1, bv1, wo1, bo1, out):
    S, T, D = x.shape
    M, C = ctx.shape[1:]
    PAIRS = S // 2
    KD, KC = D // P, C // P
    J = 2 * T // P
    RT, RM = T // P, M // P
    SCALE = float(D) ** -0.5
    assert (T, M, D, C) == (256, 256, 512, 256) and wq0.shape == (D, D)

    x_rows = x.rearrange("s t d -> (s t) d")
    ctx_rows = ctx.rearrange("s m c -> (s m) c")
    out_rows = out.rearrange("s t d -> (s t) d")

    with ExitStack() as whole:
        def sb(name, shape, dt=F32, scope=whole):
            return scope.enter_context(nc.sbuf_tensor(name, shape, dt))

        def pair(name, shape, scope=whole):
            return sb(name + "_hi", shape, F32R, scope), sb(name + "_lo", shape, F32R, scope)

        def sem(name):
            return whole.enter_context(nc.semaphore(name))

        psum = [whole.enter_context(nc.psum_tensor(f"bank{b}", [P, 512], F32)) for b in range(BANKS)]

        ident = sb("ident", [P, P])
        ones_r = sb("ones_r", [P, P], F32R)
        WQK = [pair("wqk0", [P, KD, C]), pair("wqk1", [P, KD, C])]
        WV0 = pair("wv0", [P, KC, D])
        WVO = pair("wvo", [P, KC, D])
        terms = [sb("terms0", [P, KD + KC + 1]), sb("terms1", [P, KD + KC + 1])]
        ccol = [t[:, KD:KD + KC + 1] for t in terms]
        u_b = [sb("u0_b", [P, D]), sb("u1_b", [P, D])]
        bv0_b = sb("bv0_b", [P, D])
        gamma_b = sb("gamma_b", [P, D])
        beta_b = sb("beta_b", [P, D])
        gamma_col, bv1_col = sb("gamma_col", [P, KD]), sb("bv1_col", [P, KD])
        gscale = sb("gscale", [P, KD])

        XN = [sb("x_even", [P, J, D]), sb("x_odd", [P, J, D])]
        ctxn = sb("ctxn", [P, J, C])
        XT = pair("xT", [P, KD, J * P])
        Y = pair("y", [P, KC, J * P])
        E0 = sb("e0", [P, 2, RM, T])
        N = sb("n", [P, J, D])
        rs = sb("rs", [P, J])
        prod = [sb("prod0", [P, D]), sb("prod1", [P, D])]
        bias2 = sb("bias2", [P, D])
        r0 = sb("r0", [P, J])
        r0s = sb("r0s", [P, J])
        RB = sb("rb", [P, J * P])
        bias = [prod[0], prod[1], bias2, RB]
        mx0, neg0, sum0, rinv0 = (sb(n, [P, J]) for n in ("mx0", "neg0", "sum0", "rinv0"))
        r1, mx1, top1, neg1, sum1, rinv1 = (sb(n, [P, J]) for n in ("r1", "mx1", "top1", "neg1", "sum1", "rinv1"))
        stats = sb("stats", [P, J, 6])
        mv = sb("mv", [P, J, 2])
        var_eps = sb("var_eps", [P, J])
        rstd = sb("rstd", [P, J])
        waited = sb("waited", [P, 2])
        minus_half = sb("minus_half", [P, J])
        CT_even, CN_even = pair("cT_even", [P, KC, J * P]), pair("cn_even", [P, J, C])

        with ExitStack() as stage0:
            wq0_sb = sb("wq0_sb", [P, KD, D], scope=stage0)
            wk0_sb = sb("wk0_sb", [P, KC, D], scope=stage0)
            wv0_sb = sb("wv0_sb", [P, KC, D], scope=stage0)
            wqT0 = sb("wqT0", [P, KD, D], scope=stage0)
            wkT0 = sb("wkT0", [P, KD, C], scope=stage0)
        CT_odd, CN_odd = pair("cT_odd", [P, KC, J * P]), pair("cn_odd", [P, J, C])
        W = pair("w", [P, 2, RM, T])
        WC = pair("wc", [P, 2, KC, T])
        CT, CN = [CT_even, CT_odd], [CN_even, CN_odd]
        with ExitStack() as stage1:
            wq1_sb = sb("wq1_sb", [P, KD, D], scope=stage1)
            wqT1 = sb("wqT1", [P, KD, D], scope=stage1)
            wk1_sb = sb("wk1_sb", [P, KC, D], scope=stage1)
            wkT1 = sb("wkT1", [P, KD, C], scope=stage1)
            wv1_sb = sb("wv1_sb", [P, KC, D], scope=stage1)
            wvT1 = sb("wvT1", [P, KD, C], scope=stage1)
            wo1_sb = sb("wo1_sb", [P, KD, D], scope=stage1)
            bo1_b = sb("bo1_b", [P, D], scope=stage1)
            bq0_b = sb("bq0_b", [P, D], scope=stage1)
            bk0_b = sb("bk0_b", [P, D], scope=stage1)
            bq1_b = sb("bq1_b", [P, D], scope=stage1)
            bk1_b = sb("bk1_b", [P, D], scope=stage1)
            betaq = sb("betaq", [P, KD], scope=stage1)
            dots = [sb(f"dots{n}", [P, KD + KC + 1], scope=stage1) for n in range(2)]
        NT = pair("nT", [P, KD, J * P])
        Y1 = pair("y1", [P, KC, J * P])
        PT = pair("pt", [P, 2, RM, T])
        PC = pair("pc", [P, 2, KC, T])
        E1 = sb("e1", [P, 2, RT, M])
        R = sb("r", [P, J, D])

        filled = [sem(f"filled{b}") for b in range(BANKS)]
        emptied = [sem(f"emptied{b}") for b in range(BANKS)]
        x_loaded = [sem("x_even_loaded"), sem("x_odd_loaded")]
        ctx_loaded = sem("ctx_loaded")
        ROWS = 4
        rows_in_or_stored = sem("rows_in_or_stored")
        wq0_loaded = [sem(f"wq0_block{k}_loaded") for k in range(KD)]
        loaded = {n: sem(f"{n}_loaded") for n in
                  ("wk0", "wv0", "rows0", "rows1", "cols", "wq1", "wk1", "wv1", "wo1")}
        ident_ready, consts_ready, zeroed = sem("ident_ready"), sem("consts_ready"), sem("zeroed")
        wv0_hi, wv0_ready, gscale_ready = sem("wv0_rounded"), sem("wv0_ready"), sem("gscale_ready")
        dots_ready, u_ready, c_ready = sem("dots_ready"), sem("u_ready"), sem("c_ready")
        beta_ready = sem("beta_ready")
        prep_hi = sem("prep_hi")
        hi = {n: sem(f"{n}_hi_ready") for n in ("xT", "cT", "cn", "y", "w", "wc", "nT", "y1", "pt", "pc")}
        cn_lo, w_lo = sem("cn_lo_ready"), sem("w_lo_ready")
        r0_ready, r0s_ready, exp0_ready = sem("r0_ready"), sem("r0s_ready"), sem("exp0_ready")
        mx0_ready, neg0_ready, rinv0_ready = sem("mx0_ready"), sem("neg0_ready"), sem("rinv0_ready")
        bias_ready, x_biased = sem("bias_ready"), sem("x_biased")
        stats_ready, mv_ready = sem("stats_ready"), sem("mv_ready")
        var_ready, rstd_ready, n_ready = sem("var_ready"), sem("rstd_ready"), sem("n_ready")
        prod_ready, r1_ready = sem("prod_ready"), sem("r1_ready")
        mx1_ready, top1_ready, neg1_ready, rinv1_ready = (sem("mx1_ready"), sem("top1_ready"),
                                                          sem("neg1_ready"), sem("rinv1_ready"))
        scaled_ready, resid_ready = sem("scaled_ready"), sem("resid_ready")

        block = whole.enter_context(nc.Block())

        def at(tile):
            return psum[BANK[tile]]

        def wait_filled(eng, it, name, k=0):
            eng.wait_ge(filled[BANK[name, k]], it.fill((name, k)))

        def wait_emptied(eng, it, name, k=0):
            eng.wait_ge(emptied[BANK[name, k]], it.fill((name, k)))

        def run(eng, iteration):
            iteration(Iteration(PAIRS, 0))
            with eng.Fori(0, (PAIRS - 2) // 2) as j:
                iteration(Iteration(PAIRS, 1, j))
                iteration(Iteration(PAIRS, 2, j))
            iteration(Iteration(PAIRS, PAIRS - 1))
            iteration(Iteration(PAIRS, PAIRS))

        @block.sync
        def _(sp):
            def known_early(it, value):
                if it.j is not None:
                    sp.compute_val(value)
                return value

            def rows_of(t, start):
                return t[bass.ds(start, J * P), :].rearrange("(j p) d -> p j d", p=P)

            def by_partition(v):
                return v.rearrange("(k p) -> p k", p=P)

            for k in range(KD):
                sp.dma_start(wq0_sb[:, k, :], wq0[k * P:(k + 1) * P, :]).then_inc(wq0_loaded[k], 16)
            sp.dma_start(wk0_sb[:], wk0.rearrange("(k p) e -> p k e", p=P)).then_inc(loaded["wk0"], 16)
            for t, v in ((bq0_b, bq0), (bk0_b, bk0)):
                sp.dma_start(t[:], v.partition_broadcast(P)).then_inc(loaded["rows0"], 16)
            sp.dma_start(XN[0][:], rows_of(x_rows, 0)).then_inc(x_loaded[0], 16)
            sp.dma_start(ctxn[:], rows_of(ctx_rows, 0)).then_inc(ctx_loaded, 16)
            sp.dma_start(wv0_sb[:], wv0.rearrange("(k p) e -> p k e", p=P)).then_inc(loaded["wv0"], 16)
            for t, v in ((bv0_b, bv0), (gamma_b, gamma), (beta_b, beta), (bo1_b, bo1)):
                sp.dma_start(t[:], v.partition_broadcast(P)).then_inc(rows_in_or_stored, 16)
            sp.dma_start(wq1_sb[:], wq1.rearrange("(k p) e -> p k e", p=P)).then_inc(loaded["wq1"], 16)
            for t, v in ((bq1_b, bq1), (bk1_b, bk1)):
                sp.dma_start(t[:], v.partition_broadcast(P)).then_inc(loaded["rows1"], 16)
            with nc.allow_non_contiguous_dma("two vectors, one element per partition"):
                for t, v in ((gamma_col, gamma), (bv1_col, bv1)):
                    sp.dma_start(t[:], by_partition(v)).then_inc(loaded["cols"], 16)
            sp.dma_start(wk1_sb[:], wk1.rearrange("(k p) e -> p k e", p=P)).then_inc(loaded["wk1"], 16)
            sp.dma_start(wv1_sb[:], wv1.rearrange("(k p) e -> p k e", p=P)).then_inc(loaded["wv1"], 16)
            sp.dma_start(wo1_sb[:], wo1.rearrange("(k p) e -> p k e", p=P)).then_inc(loaded["wo1"], 16)

            def iteration(it):
                more = it.j is not None or it.known < PAIRS - 1
                if more:
                    upcoming = known_early(it, it.times(J * P, J * P))
                    cT_filled = known_early(it, it.fill(("cT", KC - 1)))
                    cn_cut = known_early(it, it.times(1, 1))
                if it.back:
                    finished = known_early(it, it.times(J * P, -J * P))
                    n_made = known_early(it, it.times(J, 0))
                    out_made = [known_early(it, it.fill(("out", j))) for j in range(J)]
                if more:
                    if it.back:
                        sp.wait_ge(n_ready, n_made)
                    sp.dma_start(XN[1 - it.parity][:], rows_of(x_rows, upcoming))\
                        .then_inc(x_loaded[1 - it.parity], 16)
                    sp.wait_ge(filled[BANK["cT", KC - 1]], cT_filled)
                    sp.wait_ge(cn_lo, cn_cut)
                    sp.dma_start(ctxn[:], rows_of(ctx_rows, upcoming)).then_inc(ctx_loaded, 16)
                if it.back:
                    for j in range(J):
                        sp.wait_ge(emptied[BANK["out", j]], out_made[j])
                    sp.dma_start(rows_of(out_rows, finished), R[:]).then_inc(rows_in_or_stored, 16)

            run(sp, iteration)
            sp.wait_ge(rows_in_or_stored, 16 * (ROWS + PAIRS))

        @block.tensor
        def _(pe):
            def begin(it, name, k=0):
                n = it.fill((name, k))
                if it.j is not None or n > 1:
                    pe.wait_ge(emptied[BANK[name, k]], n - 1)
                return at((name, k))

            def end(mm, name, k=0):
                mm.then_inc(filled[BANK[name, k]], 1)

            def passes(w, m):
                return ((w[0], m[0]), (w[0], m[1]), (w[1], m[0]))

            def product(dst, terms, last=True, first=True):
                for n, (w, m) in enumerate(terms):
                    mm = pe.matmul(dst, w, m, start=first and n == 0, stop=last and n == len(terms) - 1)
                return mm

            def transposes(it, name, k, blocks):
                dst = begin(it, name, k)
                for n, src in enumerate(blocks):
                    mm = pe.transpose(dst[:, n * P:(n + 1) * P], src, ident[:])
                end(mm, name, k)

            def weight_products(it, L, wqT, wkT):
                for k in range(KD):
                    g, h = divmod(k, 2)
                    if h == 0:
                        dst = begin(it, f"wqk{L}", g)
                    for e in range(KD):
                        if k == 0:
                            wait_emptied(pe, it, f"wqT{L}", e)
                            wait_emptied(pe, it, f"wkT{L}", e // 2)
                        mm = pe.matmul(dst[:, h * C:(h + 1) * C], wqT[:, e, k * P:(k + 1) * P], wkT[:, e, :],
                                       start=e == 0, stop=e == KD - 1)
                    if h == 1:
                        end(mm, f"wqk{L}", g)

            def spread(it, name, columns):
                transposes(it, name, 0, [columns[:, k:k + 1].to_broadcast([P, P]) for k in range(KD)])

            def transpose_kv(it, name, w, arrived):
                pe.wait_ge(arrived, 16)
                for g in range(2):
                    transposes(it, name, g, [w[:, c, e * P:(e + 1) * P]
                                             for e in (2 * g, 2 * g + 1) for c in range(KC)])

            def warm_up():
                for _ in range(8):
                    pe.matmul(psum[0][:], ones_r[:], ones_r[:, 0:1].to_broadcast([P, 512]), start=True, stop=True)

            def prepare0(it):
                pe.wait_ge(ident_ready, 2)
                for k in range(KD):
                    pe.wait_ge(wq0_loaded[k], 16)
                    for e in range(KD):
                        mm = pe.transpose(at(("wqT0", e))[:, k * P:(k + 1) * P], wq0_sb[:, k, e * P:(e + 1) * P],
                                          ident[:])
                        if k == KD - 1:
                            end(mm, "wqT0", e)
                transpose_kv(it, "wkT0", wk0_sb, loaded["wk0"])
                weight_products(it, 0, wqT0, wkT0)
                pe.wait_ge(u_ready, 1)
                spread(it, "u0", terms[0])

            def prepare1a(it):
                pe.wait_ge(loaded["wq1"], 16)
                for e in range(KD):
                    transposes(it, "wqT1", e, [wq1_sb[:, k, e * P:(e + 1) * P] for k in range(KD)])
                transpose_kv(it, "wkT1", wk1_sb, loaded["wk1"])

            def prepare1b(it):
                transpose_kv(it, "wvT1", wv1_sb, loaded["wv1"])
                weight_products(it, 1, wqT1, wkT1)
                pe.wait_ge(dots_ready, (KD + KC + 1) + KD)
                spread(it, "q1", betaq)
            def prepare1c(it):
                pe.wait_ge(u_ready, 2)
                spread(it, "u1", terms[1])
                for g in range(2):
                    wait_emptied(pe, it, "wvT1", g)
                pe.wait_ge(loaded["wo1"], 16)
                pe.wait_ge(loaded["cols"], 16 * 2)
                for c in range(KC):
                    dst = begin(it, "wvo", c)
                    end(product(dst[:, :D], [(wvT1[:, h, c * P:(c + 1) * P], wo1_sb[:, h, :])
                                             for h in range(KD)]), "wvo", c)
                dst = begin(it, "bo1")
                end(product(dst[:, :D], [(bv1_col[:, h:h + 1].to_broadcast([P, P]), wo1_sb[:, h, :])
                                         for h in range(KD)]), "bo1")

            def transpose_inputs(it):
                xn = XN[it.parity]
                pe.wait_ge(x_loaded[it.parity], it.loads())
                for k in range(KD):
                    transposes(it, "xT", k, [xn[:, j, k * P:(k + 1) * P] for j in range(J)])
                pe.wait_ge(ctx_loaded, it.times(16, 16))
                for c in range(KC):
                    transposes(it, "cT", c, [ctxn[:, j, c * P:(c + 1) * P] for j in range(J)])

            def transpose_n(it):
                pe.wait_ge(n_ready, it.times(J, 0))
                for k in range(KD):
                    transposes(it, "nT", k, [N[:, j, k * P:(k + 1) * P] for j in range(J)])

            def project(it, name, source, wqk, src):
                dst = [begin(it, name, c) for c in range(KC)]
                for k in range(KD):
                    wait_emptied(pe, it, source, k)
                    for c in range(KC):
                        w = [h[:, k, c * P:(c + 1) * P] for h in wqk]
                        mm = product(dst[c][:], passes(w, [h[:, k, :] for h in src]),
                                     first=k == 0, last=k == KD - 1)
                        if k == KD - 1:
                            end(mm, name, c)

            def spread_r0(it):
                pe.wait_ge(r0s_ready, it.times(1, 1))
                spread(it, "rb", r0s)

            def scores0(it):
                ct = CT[it.parity]
                for c in range(KC):
                    wait_emptied(pe, it, "y", c)
                for c in range(KC):
                    wait_emptied(pe, it, "cT", c)
                for b in range(2):
                    dst = begin(it, "s0", b)
                    for mt in range(RM):
                        m0 = b * M + mt * P
                        part = dst[:, mt * T:(mt + 1) * T]
                        terms = []
                        for c in range(KC):
                            terms += passes([h[:, c, m0:m0 + P] for h in ct],
                                            [h[:, c, b * T:(b + 1) * T] for h in Y])
                        mm = product(part, terms)
                    end(mm, "s0", b)

            def scores1(it):
                ct = CT[1 - it.parity]
                for c in range(KC):
                    wait_emptied(pe, it, "y1", c)
                for b in range(2):
                    dst = begin(it, "s1", b)
                    for tt in range(RT):
                        t0 = b * T + tt * P
                        terms = []
                        for c in range(KC):
                            terms += passes([h[:, c, t0:t0 + P] for h in Y1],
                                            [h[:, c, b * M:(b + 1) * M] for h in ct])
                        mm = product(dst[:, tt * M:(tt + 1) * M], terms)
                    end(mm, "s1", b)

            def weigh(it, name, b, cn, probs):
                dst = begin(it, name, b)
                for ct in range(KC):
                    terms = []
                    for mt in range(RM):
                        terms += passes([h[:, b * RM + mt, ct * P:(ct + 1) * P] for h in cn],
                                        [h[:, b, mt, :] for h in probs])
                    mm = product(dst[:, ct * T:(ct + 1) * T], terms)
                end(mm, name, b)

            def weigh0(it, b):
                if b == 0:
                    pe.wait_ge(cn_lo, it.times(1, 1))
                weigh(it, "wc", b, CN[it.parity], W)

            def row_sums(it):
                pe.wait_ge(w_lo, it.times(2 * RM, 2 * RM))
                dst = begin(it, "rs")
                end(product(dst[:], [(ones_r[:], h[:, :, mt, :]) for mt in range(RM) for h in W]), "rs")

            def transpose_probs(it, b):
                wait_emptied(pe, it, "s1", b)
                transposes(it, "pt", b, [E1[:, b, tt, mt * P:(mt + 1) * P] for mt in range(RM) for tt in range(RT)])

            def apply(it, name, source, j, left, right):
                b, tt = divmod(j, RT)
                if tt == 0:
                    wait_emptied(pe, it, source, b)
                dst = begin(it, name, j)
                terms = []
                for ct in range(KC):
                    terms += passes([h[:, b, ct, tt * P:(tt + 1) * P] for h in left], [h[:, ct, :] for h in right])
                end(product(dst[:], terms), name, j)

            def iteration(it):
                begin_it = it.j is None and it.known == 0
                if begin_it:
                    prepare0(it)
                if it.front:
                    transpose_inputs(it)
                    project(it, "y", "xT", WQK[0], XT)
                if begin_it:
                    prepare1a(it)
                if it.back:
                    transpose_n(it)
                if it.front:
                    spread_r0(it)
                    scores0(it)
                if begin_it:
                    prepare1b(it)
                if it.back:
                    project(it, "y1", "nT", WQK[1], NT)
                if it.front:
                    row_sums(it)
                    weigh0(it, 0)
                    weigh0(it, 1)
                if it.back:
                    scores1(it)
                if it.front:
                    if begin_it:
                        pe.wait_ge(wv0_ready, 1)
                    apply(it, "pr", "wc", 0, WC, WV0)
                    apply(it, "pr", "wc", 1, WC, WV0)
                if it.back:
                    transpose_probs(it, 0)
                    transpose_probs(it, 1)
                for b in range(2):
                    if it.front:
                        apply(it, "pr", "wc", 2 + b, WC, WV0)
                    if it.back:
                        wait_emptied(pe, it, "pt", b)
                        weigh(it, "pc", b, CN[1 - it.parity], PT)
                if begin_it:
                    prepare1c(it)
                if it.back:
                    for j in range(J):
                        apply(it, "out", "pc", j, PC, WVO)

            pe.wait_ge(consts_ready, 1)
            warm_up()
            run(pe, iteration)

        @block.scalar
        def _(act):
            def round_bank(it, name, k, dst, bias=None, scale=None):
                wait_filled(act, it, name, k)
                if bias is not None:
                    i = act.activation(dst, at((name, k))[:], ACT.Identity, bias=bias)
                elif scale is not None:
                    i = act.activation(dst, at((name, k))[:], ACT.Copy, scale=scale)
                else:
                    i = act.activation(dst, at((name, k))[:], ACT.Copy)
                i.then_inc(hi[name] if name in hi else prep_hi, 1)

            def prep_copy(it, name, k, dst, scale=1.0):
                wait_filled(act, it, name, k)
                src = at((name, k))[:, 0:dst.free_size()] if len(dst.shape) == 2 else at((name, k))[:]
                act.activation(dst, src, ACT.Copy, scale=scale).then_inc(emptied[BANK[name, k]], 1)

            def two(t, g):
                return t[:, 2 * g:2 * g + 2, :].rearrange("p k c -> p (k c)")

            def round_weights(it, L, k, scale):
                g, h = divmod(k, 2)
                wait_filled(act, it, f"wqk{L}", g)
                act.activation(WQK[L][0][:, k, :], at((f"wqk{L}", g))[:, h * C:(h + 1) * C], ACT.Copy,
                               scale=scale).then_inc(prep_hi, 1)

            def prepare0(it):
                for e in (0, 2):
                    prep_copy(it, "wqT0", e, wqT0[:, e, :])
                prep_copy(it, "wkT0", 0, two(wkT0, 0))
                for k in range(KD):
                    round_weights(it, 0, k, SCALE)
                prep_copy(it, "u0", 0, u_b[0][:])

            def prepare1a(it):
                for e in range(KD):
                    prep_copy(it, "wqT1", e, wqT1[:, e, :])
                for g in range(2):
                    prep_copy(it, "wkT1", g, two(wkT1, g))

            def prepare1b(it):
                for g in range(2):
                    prep_copy(it, "wvT1", g, two(wvT1, g))
                act.wait_ge(gscale_ready, 1)
                for k in range(KD):
                    round_weights(it, 1, k, gscale[:, k:k + 1])

            def cut_v0(it):
                act.wait_ge(loaded["wv0"], 16)
                act.activation(WV0[0][:], wv0_sb[:], ACT.Copy).then_inc(wv0_hi, 1)

            def prepare1c(it):
                prep_copy(it, "u1", 0, u_b[1][:])
                for c in range(KC):
                    round_bank(it, "wvo", c, WVO[0][:, c, :])

            def softmax0(it):
                for b in range(2):
                    act.wait_ge(neg0_ready, it.times(2, b + 1))
                    for mt in range(RM):
                        q = b * RM + mt
                        e = act.activation(E0[:, b, mt, :], E0[:, b, mt, :], ACT.Exp,
                                           bias=neg0[:, q:q + 1], accum_out=sum0[:, q:q + 1])
                    e.then_inc(exp0_ready, 1)
                for b in range(2):
                    act.wait_ge(rinv0_ready, it.times(2, b + 1))
                    for mt in range(RM):
                        q = b * RM + mt
                        act.activation(W[0][:, b, mt, :], E0[:, b, mt, :], ACT.Copy,
                                       scale=rinv0[:, q:q + 1]).then_inc(hi["w"], 1)

            def softmax1(it):
                for b in range(2):
                    act.wait_ge(neg1_ready, it.times(2, b - 1))
                    for tt in range(RT):
                        q = b * RT + tt
                        e = act.activation(E1[:, b, tt, :], at(("s1", b))[:, tt * M:(tt + 1) * M], ACT.Exp,
                                           bias=neg1[:, q:q + 1], accum_out=sum1[:, q:q + 1])
                    e.then_inc(emptied[BANK["s1", b]], 1)

            def bias_of_rows(it, j):
                wait_emptied(act, it, "rs")
                act.activation(bias[j][:], bv0_b[:], ACT.Copy, scale=rs[:, j:j + 1]).then_inc(bias_ready, 1)

            def row_terms(it, blocks):
                for j in blocks:
                    act.wait_ge(prod_ready, it.times(J, j + 1 - J))
                    act.activation(prod[j % 2][:], prod[j % 2][:], ACT.Copy,
                                   accum_out=r1[:, j:j + 1]).then_inc(r1_ready, 1)

            def halves(t, b):
                return t[:, b].rearrange("p k t -> p (k t)")

            def iteration(it):
                begin_it = it.j is None and it.known == 0
                if begin_it:
                    prepare0(it)
                if it.front:
                    for k in range(KD):
                        round_bank(it, "xT", k, XT[0][:, k, :])
                    for c in range(KC):
                        round_bank(it, "cT", c, CT[it.parity][0][:, c, :])
                    act.wait_ge(ctx_loaded, it.times(16, 16))
                    act.activation(CN[it.parity][0][:], ctxn[:], ACT.Copy).then_inc(hi["cn"], 1)
                    if begin_it:
                        cut_v0(it)
                    for c in range(KC):
                        round_bank(it, "y", c, Y[0][:, c, :], bias=ccol[0][:, c:c + 1])
                if begin_it:
                    prepare1a(it)
                if it.back:
                    for k in range(KD):
                        round_bank(it, "nT", k, NT[0][:, k, :])
                if it.front:
                    prep_copy(it, "rb", 0, RB[:])
                if it.back:
                    row_terms(it, (0, 1))
                if it.front:
                    softmax0(it)
                if begin_it:
                    prepare1b(it)
                if it.back:
                    row_terms(it, (2, 3))
                    for c in range(KC):
                        round_bank(it, "y1", c, Y1[0][:, c, :], bias=ccol[1][:, c:c + 1])
                if it.front:
                    if begin_it:
                        act.wait_ge(rows_in_or_stored, 16 * ROWS)
                    for b in range(2):
                        round_bank(it, "wc", b, halves(WC[0], b))
                        bias_of_rows(it, b)
                    for j in range(2, J):
                        bias_of_rows(it, j)
                if it.back:
                    softmax1(it)
                if begin_it:
                    prepare1c(it)
                if it.back:
                    for b in range(2):
                        round_bank(it, "pt", b, halves(PT[0], b))
                    for b in range(2):
                        round_bank(it, "pc", b, halves(PC[0], b))

            run(act, iteration)

        @block.vector
        def _(dve):
            rounded = {"prep": 0, "dots": 0}

            def low(it, name, k, dst, high, bias=None, scale=None, per=0, back=0):
                dve.wait_ge(hi[name], it.times(per, k + 1 - back * per))
                src = at((name, k))[:]
                if bias is not None:
                    i = dve.scalar_tensor_tensor(dst, src, bias, high.bitcast(F32), ALU.add, ALU.subtract)
                else:
                    i = dve.tensor_tensor(dst, src, high.bitcast(F32), ALU.subtract)
                i.then_inc(emptied[BANK[name, k]], 1)

            def low_weights(it, name, k, parts, bank_parts, scales):
                rounded["prep"] += len(parts)
                dve.wait_ge(prep_hi, rounded["prep"])
                for (high, lo), src, scale in zip(parts, bank_parts, scales):
                    i = dve.scalar_tensor_tensor(lo, src, scale, high.bitcast(F32), ALU.mult, ALU.subtract)
                i.then_inc(emptied[BANK[name, k]], 1)

            def low_wqk(it, L, scale_of):
                for g in range(KD // 2):
                    bank = at((f"wqk{L}", g))
                    low_weights(it, f"wqk{L}", g, [[h[:, 2 * g + n, :] for h in WQK[L]] for n in range(2)],
                                [bank[:, n * C:(n + 1) * C] for n in range(2)],
                                [scale_of(2 * g + n) for n in range(2)])

            def dot(dst, a, b):
                n = rounded["dots"]
                rounded["dots"] += 1
                if n >= J:
                    dve.wait_ge(dots_ready, n - J + 1)
                i = dve.tensor_tensor_reduce(N[:, n % J, :], a, b, 1.0, 0.0, ALU.mult, ALU.add, dst)
                i.then_inc(dots_ready, 1)

            def dots_done():
                dve.wait_ge(dots_ready, rounded["dots"])

            def wq_bk(L, wq, bk):
                for k in range(KD):
                    dot(dots[L][:, k:k + 1], wq[:, k, :], bk[:])

            def wk_bq(L, wk, bq, bk):
                for c in range(KC):
                    dot(dots[L][:, KD + c:KD + c + 1], wk[:, c, :], bq[:])
                dot(dots[L][:, KD + KC:], bk[:], bq[:])
                dots_done()
                dve.tensor_scalar(ccol[L], dots[L][:, KD:], SCALE, None, ALU.mult).then_inc(c_ready, 1)

            def prepare0(it):
                for e in (1, 3):
                    wait_filled(dve, it, "wqT0", e)
                    dve.tensor_copy(wqT0[:, e, :], at(("wqT0", e))[:]).then_inc(emptied[BANK["wqT0", e]], 1)
                wait_filled(dve, it, "wkT0", 1)
                dve.tensor_copy(wkT0[:, 2:4, :].rearrange("p k c -> p (k c)"), at(("wkT0", 1))[:])\
                   .then_inc(emptied[BANK["wkT0", 1]], 1)
                dve.wait_ge(loaded["rows0"], 16 * 2)
                dve.wait_ge(loaded["wk0"], 16)
                wk_bq(0, wk0_sb, bq0_b, bk0_b)
                for k in range(KD):
                    dve.wait_ge(wq0_loaded[k], 16)
                wq_bk(0, wq0_sb, bk0_b)
                dots_done()
                dve.tensor_scalar(terms[0][:, :KD], dots[0][:, :KD], SCALE, None, ALU.mult).then_inc(u_ready, 1)
                low_wqk(it, 0, lambda k: SCALE)

            def prepare1a(it):
                dve.wait_ge(loaded["cols"], 16 * 2)
                dve.tensor_scalar(gscale[:], gamma_col[:], SCALE, None, ALU.mult).then_inc(gscale_ready, 1)

            def cut_v0(it):
                dve.wait_ge(wv0_hi, 1)
                dve.tensor_tensor(WV0[1][:], wv0_sb[:], WV0[0][:].bitcast(F32), ALU.subtract).then_inc(wv0_ready, 1)

            def row_terms1(it):
                dve.wait_ge(loaded["wq1"], 16)
                dve.wait_ge(loaded["rows1"], 16 * 2)
                wq_bk(1, wq1_sb, bk1_b)
                dots_done()
                dve.wait_ge(gscale_ready, 1)
                dve.tensor_tensor(terms[1][:, :KD], dots[1][:, :KD], gscale[:], ALU.mult).then_inc(u_ready, 1)

            def beta_wq1(it):
                dve.wait_ge(rows_in_or_stored, 16 * ROWS)
                for e in range(KD):
                    wait_emptied(dve, it, "wqT1", e)
                    dot(betaq[:, e:e + 1], wqT1[:, e, :], beta_b[:])
                dots_done()

            def prepare1b(it):
                low_wqk(it, 1, lambda k: gscale[:, k:k + 1])
                wait_filled(dve, it, "q1")
                dve.tensor_tensor(bq1_b[:], at(("q1", 0))[:], bq1_b[:], ALU.add).then_inc(emptied[BANK["q1", 0]], 1)

            def column_terms1(it):
                wait_emptied(dve, it, "q1")
                dve.wait_ge(loaded["wk1"], 16)
                wk_bq(1, wk1_sb, bq1_b, bk1_b)

            def prepare1c(it):
                for c in range(KC):
                    low_weights(it, "wvo", c, [[h[:, c, :] for h in WVO]], [at(("wvo", c))[:]], [1.0])
                wait_filled(dve, it, "bo1")
                dve.wait_ge(rows_in_or_stored, 16 * ROWS)
                dve.tensor_tensor(bo1_b[:], at(("bo1", 0))[:, 0:D], bo1_b[:], ALU.add)\
                   .then_inc(emptied[BANK["bo1", 0]], 1)
                wait_emptied(dve, it, "bo1")
                dve.tensor_tensor(beta_b[:], beta_b[:], bo1_b[:], ALU.add).then_inc(beta_ready, 1)

            def row_terms0(it):
                dve.wait_ge(x_loaded[it.parity], it.loads())
                if it.j is None and it.known == 0:
                    wait_emptied(dve, it, "u0")
                for j in range(J):
                    if it.j is not None or it.known or j:
                        dve.wait_ge(r0_ready, it.times(J, j))
                    dve.tensor_tensor_reduce(RB[:], XN[it.parity][:, j, :], u_b[0][:], 1.0, 0.0, ALU.mult,
                                             ALU.add, r0[:, j:j + 1]).then_inc(r0_ready, 1)
                dve.wait_ge(r0_ready, it.times(J, J))
                dve.tensor_scalar(r0s[:], r0[:], ccol[0][:, KC:KC + 1], None, ALU.add).then_inc(r0s_ready, 1)

            def maxima0(it):
                for b in range(2):
                    if b == 0:
                        wait_emptied(dve, it, "rb")
                    wait_filled(dve, it, "s0", b)
                    dve.memset(waited[:, b:b + 1], 0.0)
                    for mt in range(RM):
                        q = b * RM + mt
                        i = dve.tensor_tensor_reduce(E0[:, b, mt, :], at(("s0", b))[:, mt * T:(mt + 1) * T],
                                                     RB[:, b * T:(b + 1) * T], 1.0, LOWEST, ALU.add, ALU.max,
                                                     mx0[:, q:q + 1])
                        i.then_inc(*((emptied[BANK["s0", b]], 1) if mt == RM - 1 else (mx0_ready, 1)))
                    dve.wait_ge(mx0_ready, it.times(2, b + 1))
                    wait_emptied(dve, it, "s0", b)
                    q = slice(b * RM, (b + 1) * RM)
                    dve.tensor_scalar(neg0[:, q], mx0[:, q], -1.0, None, ALU.mult).then_inc(neg0_ready, 1)

            def maxima1(it):
                s = ccol[1][:, KC:KC + 1]
                dve.wait_ge(r1_ready, it.times(J, 0))
                for b in range(2):
                    wait_filled(dve, it, "s1", b)
                    q = slice(b * RT, (b + 1) * RT)
                    dve.tensor_reduce(mx1[:, q], at(("s1", b))[:].rearrange("p (t m) -> p t m", t=RT), AX_X,
                                      ALU.max).then_inc(mx1_ready, 1)
                    dve.wait_ge(mx1_ready, it.times(2, b - 1))
                    dve.scalar_tensor_tensor(top1[:, q], r1[:, q], s, mx1[:, q], ALU.add, ALU.add)\
                       .then_inc(top1_ready, 1)
                    dve.wait_ge(top1_ready, it.times(2, b - 1))
                    dve.scalar_tensor_tensor(neg1[:, q], r1[:, q], s, top1[:, q], ALU.add, ALU.subtract)\
                       .then_inc(neg1_ready, 1)

            def normalise0(it):
                for b in range(2):
                    dve.wait_ge(exp0_ready, it.times(2, b + 1))
                    q = slice(b * RM, (b + 1) * RM)
                    dve.reciprocal(rinv0[:, q], sum0[:, q]).then_inc(rinv0_ready, 1)
                for b in range(2):
                    for mt in range(RM):
                        q = b * RM + mt
                        dve.wait_ge(hi["w"], it.times(2 * RM, q + 1))
                        dve.scalar_tensor_tensor(W[1][:, b, mt, :], E0[:, b, mt, :], rinv0[:, q:q + 1],
                                                 W[0][:, b, mt, :].bitcast(F32), ALU.mult, ALU.subtract)\
                           .then_inc(w_lo, 1)

            def norm_and_output(it):
                xn = XN[it.parity]

                def add(j):
                    wait_filled(dve, it, "pr", j)
                    dve.wait_ge(x_biased, it.times(J, j + 1))
                    dve.tensor_tensor(xn[:, j, :], at(("pr", j))[:], xn[:, j, :], ALU.add)\
                       .then_inc(emptied[BANK["pr", j]], 1)

                def statistics(j):
                    wait_emptied(dve, it, "pr", j)
                    dve.bn_stats(stats[:, j, :], xn[:, j, :]).then_inc(stats_ready, 1)

                def aggregate(b):
                    for j in range(b * RT, (b + 1) * RT):
                        dve.bn_aggr(mv[:, j, :], stats[:, j, :]).then_inc(mv_ready, 1)
                    dve.wait_ge(mv_ready, it.times(J, (b + 1) * RT))
                    q = slice(b * RT, (b + 1) * RT)
                    dve.tensor_scalar(var_eps[:, q], mv[:, q, 1], EPS, None, ALU.add).then_inc(var_ready, 1)

                def normalise(j):
                    dve.wait_ge(rstd_ready, it.times(2, j // RT + 1))
                    dve.tensor_scalar(N[:, j, :], xn[:, j, :], mv[:, j, 0:1], rstd[:, j:j + 1], ALU.subtract,
                                      ALU.mult).then_inc(n_ready, 1)

                def output(j):
                    wait_filled(dve, it, "out", j)
                    dve.wait_ge(resid_ready, it.times(J, j + 1 - J))
                    dve.scalar_tensor_tensor(R[:, j, :], at(("out", j))[:], rinv1[:, j:j + 1], R[:, j, :],
                                             ALU.mult, ALU.add).then_inc(emptied[BANK["out", j]], 1)

                def cut_pc(b):
                    low(it, "pc", b, halves(PC[1], b), halves(PC[0], b), per=2, back=1)

                def cut_pt(b):
                    low(it, "pt", b, halves(PT[1], b), halves(PT[0], b), per=2, back=1)

                if it.front:
                    add(0)
                    statistics(0)
                    add(1)
                if it.back:
                    cut_pt(0)
                    cut_pt(1)
                if it.front:
                    statistics(1)
                if it.back:
                    wait_emptied(dve, it, "s1", 1)
                    dve.reciprocal(rinv1[:], sum1[:]).then_inc(rinv1_ready, 1)
                if it.front:
                    dve.wait_ge(stats_ready, it.times(J, RT))
                    add(2)
                    aggregate(0)
                    statistics(2)
                if it.back:
                    cut_pc(0)
                if it.front:
                    if it.back:
                        wait_filled(dve, it, "nT", KD - 1)
                        dve.wait_ge(scaled_ready, it.times(J, 0))
                    normalise(0)
                    normalise(1)
                    add(3)
                    statistics(3)
                if it.back:
                    cut_pc(1)
                    dve.wait_ge(rinv1_ready, it.times(1, 0))
                    output(0)
                if it.front:
                    dve.wait_ge(stats_ready, it.times(J, J))
                    if it.back:
                        output(1)
                    aggregate(1)
                if it.back:
                    if not it.front:
                        output(1)
                    output(2)
                if it.front:
                    normalise(2)
                    normalise(3)
                if it.back:
                    output(3)

            def halves(t, b):
                return t[:, b].rearrange("p k t -> p (k t)")

            def iteration(it):
                begin_it = it.j is None and it.known == 0
                if begin_it:
                    prepare0(it)
                if it.front:
                    for k in range(KD):
                        low(it, "xT", k, XT[1][:, k, :], XT[0][:, k, :], per=KD)
                    for c in range(KC):
                        low(it, "cT", c, CT[it.parity][1][:, c, :], CT[it.parity][0][:, c, :], per=KC)
                    row_terms0(it)
                    for c in range(KC):
                        low(it, "y", c, Y[1][:, c, :], Y[0][:, c, :], bias=ccol[0][:, c:c + 1], per=KC)
                if begin_it:
                    prepare1a(it)
                    cut_v0(it)
                if it.back:
                    for k in range(KD):
                        low(it, "nT", k, NT[1][:, k, :], NT[0][:, k, :], per=KD, back=1)
                if it.front:
                    maxima0(it)
                if begin_it:
                    beta_wq1(it)
                if it.front:
                    normalise0(it)
                if begin_it:
                    row_terms1(it)
                    prepare1b(it)
                if it.back:
                    for c in range(KC):
                        low(it, "y1", c, Y1[1][:, c, :], Y1[0][:, c, :], bias=ccol[1][:, c:c + 1], per=KC, back=1)
                if it.front:
                    wait_filled(dve, it, "rs")
                    for j in range(J):
                        q = slice(j * P, (j + 1) * P)
                        i = dve.tensor_tensor_reduce(halves(E0, 0)[:, q], at(("rs", 0))[:, q], ident[:], 1.0, 0.0, ALU.mult,
                                                     ALU.add, rs[:, j:j + 1])
                    i.then_inc(emptied[BANK["rs", 0]], 1)
                    for b in range(2):
                        low(it, "wc", b, halves(WC[1], b), halves(WC[0], b), per=2)
                if begin_it:
                    column_terms1(it)
                if it.back:
                    maxima1(it)
                norm_and_output(it)
                if begin_it:
                    prepare1c(it)

            run(dve, iteration)

        @block.gpsimd
        def _(pool):
            pool.memset(ones_r[:].bitcast(F32), 1.0).then_inc(consts_ready, 1)
            pool.memset(ident[:], 0.0).then_inc(ident_ready, 1)
            pool.wait_ge(ident_ready, 1)
            pool.affine_select(out=ident[:], in_=ident[:], compare_op=ALU.not_equal, fill=1.0, base=0,
                               pattern=[[-1, P]], channel_multiplier=1).then_inc(ident_ready, 1)
            pool.memset(minus_half[:], -0.5).then_inc(consts_ready, 1)
            pool.wait_ge(consts_ready, 2)

            def cut_ctx(it):
                pool.wait_ge(hi["cn"], it.times(1, 1))
                pool.tensor_tensor(CN[it.parity][1][:], ctxn[:], CN[it.parity][0][:].bitcast(F32), ALU.subtract)\
                    .then_inc(cn_lo, 1)

            def rstds(it):
                for b in range(2):
                    pool.wait_ge(var_ready, it.times(2, b + 1))
                    q = slice(b * RT, (b + 1) * RT)
                    pool.tensor_tensor(rstd[:, q], var_eps[:, q], minus_half[:, q], ALU.pow).then_inc(rstd_ready, 1)

            def row_products(it, blocks):
                for j in blocks:
                    pool.wait_ge(n_ready, it.times(J, j + 1 - J))
                    if j >= 2:
                        pool.wait_ge(r1_ready, it.times(J, j - 1 - J))
                    pool.tensor_tensor(prod[j % 2][:], N[:, j, :], u_b[1][:], ALU.mult).then_inc(prod_ready, 1)

            def add_bias(it):
                xn = XN[it.parity]
                for j in range(J):
                    pool.wait_ge(bias_ready, it.times(J, j + 1))
                    pool.tensor_tensor(xn[:, j, :], bias[j][:], xn[:, j, :], ALU.add).then_inc(x_biased, 1)

            def scale_n(it):
                pool.wait_ge(rows_in_or_stored, it.times(16, 16 * (ROWS - 1)))
                for j in range(J):
                    pool.tensor_tensor(R[:, j, :], N[:, j, :], gamma_b[:], ALU.mult).then_inc(scaled_ready, 1)

            def add_beta(it, blocks):
                for j in blocks:
                    pool.wait_ge(scaled_ready, it.times(J, j + 1 - J))
                    pool.tensor_tensor(R[:, j, :], R[:, j, :], beta_b[:], ALU.add).then_inc(resid_ready, 1)

            def iteration(it):
                if it.front:
                    cut_ctx(it)
                if it.back:
                    row_products(it, (0, 1))
                    if it.front:
                        scale_n(it)
                    row_products(it, (2, 3))
                    if not it.front:
                        scale_n(it)
                    add_beta(it, (0, 1))
                if it.front:
                    add_bias(it)
                if it.back:
                    add_beta(it, (2, 3))
                if it.front:
                    rstds(it)

            def guarded(it):
                if it.j is None and it.known == 0:
                    iteration(it)
                    wait_emptied(pool, it, "u1")
                    pool.wait_ge(beta_ready, 1)
                else:
                    iteration(it)

            run(pool, guarded)


_INS = ['x', 'ctx_512', 'L0_xattn_Wq', 'L0_xattn_bq', 'L0_xattn_Wk', 'L0_xattn_bk', 'L0_xattn_Wv', 'L0_xattn_bv',
        'L0_xattn_gamma', 'L0_xattn_beta', 'L1_xattn_Wq', 'L1_xattn_bq', 'L1_xattn_Wk', 'L1_xattn_bk',
        'L1_xattn_Wv', 'L1_xattn_bv', 'L1_xattn_Wo', 'L1_xattn_bo']


def kernel(**inputs):
    import numpy as _np
    import concourse.bacc as _bacc
    from concourse import mybir as _mybir
    from concourse.bass_utils import run_bass_kernel_spmd as _run

    nc = _bacc.Bacc("TRN2", target_bir_lowering=False, num_devices=1)
    arrays, args = {}, []
    for name in _INS:
        a = _np.ascontiguousarray(inputs[name])
        arrays[f"in_{name}_dram"] = a
        args.append(nc.dram_tensor(f"in_{name}_dram", a.shape, _mybir.dt.from_np(a.dtype), kind="ExternalInput").ap())
    args.append(nc.dram_tensor("out_0_dram", inputs['x'].shape, _mybir.dt.float32, kind="ExternalOutput").ap())
    two_cross_attentions(nc, *args)
    r = _run(nc, [arrays], core_ids=[0])
    return r.results[0]["out_0_dram"]
```

```python
from contextlib import ExitStack

import concourse.bass as bass
from concourse import mybir

F32 = mybir.dt.float32
F32R = mybir.dt.float32r
ALU = mybir.AluOpType
ACT = mybir.ActivationFunctionType
AX_X = mybir.AxisListType.X
P = 128
BANKS = 8
LOWEST = -3.4028235e38
EPS = 1e-6

FRONT = {"xT", "cT", "rb", "y", "s0", "rs", "wc", "pr"}


def tiles(name, n):
    return [(name, k) for k in range(n)]


STEADY = (tiles("xT", 4) + tiles("cT", 2) + tiles("y", 2) + tiles("nT", 4) + tiles("rb", 1) + tiles("s0", 2)
          + tiles("y1", 2) + [("wc", 0), ("rs", 0), ("wc", 1)] + tiles("s1", 2) + tiles("pr", 2) + tiles("pt", 2)
          + [("pr", 2), ("pc", 0), ("pr", 3), ("pc", 1)] + tiles("out", 4))
PREP0 = tiles("wqT0", 4) + tiles("wkT0", 2) + tiles("wqk0", 2) + tiles("u0", 1)
PREP1A = tiles("wqT1", 4) + tiles("wkT1", 2)
PREP1B = tiles("wvT1", 2) + tiles("wqk1", 2) + tiles("q1", 1)
PREP1C = [("u1", 0), ("wvo", 0), ("bo1", 0), ("wvo", 1)]
PREP_BANKS = (7, 0, 1, 2, 3, 4, 5, 6, 7) + (0, 1, 2, 3, 4, 5) + (6, 7, 2, 3, 6) + (3, 6, 4, 7)


def place_banks():
    bank, turn = {}, 0
    for t in STEADY:
        if t[0] in ("rb", "rs"):
            bank[t] = (turn + (3 if t[0] == "rb" else 4)) % BANKS
        else:
            bank[t] = turn % BANKS
            turn += 1
    bank.update(zip(PREP0 + PREP1A + PREP1B + PREP1C, PREP_BANKS))
    return bank


BANK = place_banks()


def front_only(order):
    return [t for t in order if t[0] in FRONT]


def insert_after(order, tile, extra):
    at = order.index(tile) + 1
    return order[:at] + extra + order[at:]


FIRST = insert_after(insert_after(insert_after(front_only(STEADY), ("y", 1), PREP1A), ("s0", 1), PREP1B),
                     ("pr", 3), PREP1C)
FIRST = PREP0 + FIRST
LATE = (2, 3)
BANK["late", 2], BANK["late", 3] = 0, 1
BEFORE_LAST = [t for t in STEADY if t[0] != "out" or t[1] not in LATE]
LAST = insert_after([t for t in STEADY if t[0] not in FRONT], ("y1", 1), [("late", 2)])
LAST = insert_after(LAST, ("s1", 1), [("late", 3)])


class Iteration:

    def __init__(self, pairs, known, j=None):
        self.pairs, self.known, self.j = pairs, known, j
        self.front = j is not None or known < pairs
        self.back = j is not None or known > 0
        self.parity = known % 2
        self.before_last, self.last = j is None and known == pairs - 1, j is None and known == pairs

    def times(self, per, plus):
        return self.known * per + plus if self.j is None else self.j * (2 * per) + (self.known * per + plus)

    def loads(self):
        n = 16 * (self.known // 2 + 1)
        return n if self.j is None else self.j * 16 + n

    def fill(self, tile):
        b = BANK[tile]

        def upto(order, end):
            return sum(1 for t in order[:end] if BANK[t] == b)

        if self.j is None and self.known == 0:
            return upto(FIRST, FIRST.index(tile) + 1)
        first, steady = upto(FIRST, len(FIRST)), upto(STEADY, len(STEADY))
        if self.last:
            before = first + (self.known - 2) * steady + upto(BEFORE_LAST, len(BEFORE_LAST))
            return before + upto(LAST, LAST.index(tile) + 1)
        return self.times(steady, first - steady + upto(STEADY, STEADY.index(tile) + 1))


def two_cross_attentions(nc, x, ctx, wq0, bq0, wk0, bk0, wv0, bv0, gamma, beta,
                         wq1, bq1, wk1, bk1, wv1, bv1, wo1, bo1, out):
    S, T, D = x.shape
    M, C = ctx.shape[1:]
    PAIRS = S // 2
    KD, KC = D // P, C // P
    J = 2 * T // P
    RT, RM = T // P, M // P
    SCALE = float(D) ** -0.5
    assert (T, M, D, C) == (256, 256, 512, 256) and wq0.shape == (D, D)

    x_rows = x.rearrange("s t d -> (s t) d")
    ctx_rows = ctx.rearrange("s m c -> (s m) c")
    out_rows = out.rearrange("s t d -> (s t) d")

    with ExitStack() as whole:
        def sb(name, shape, dt=F32, scope=whole):
            return scope.enter_context(nc.sbuf_tensor(name, shape, dt))

        def pair(name, shape, scope=whole):
            return sb(name + "_hi", shape, F32R, scope), sb(name + "_lo", shape, F32R, scope)

        def sem(name):
            return whole.enter_context(nc.semaphore(name))

        psum = [whole.enter_context(nc.psum_tensor(f"bank{b}", [P, 512], F32)) for b in range(BANKS)]

        ident = sb("ident", [P, P])
        ones_r = sb("ones_r", [P, P], F32R)
        WQK = [pair("wqk0", [P, KD, C]), pair("wqk1", [P, KD, C])]
        WV0 = pair("wv0", [P, KC, D])
        WVO = pair("wvo", [P, KC, D])
        terms = [sb("terms0", [P, KD + KC + 1]), sb("terms1", [P, KD + KC + 1])]
        ccol = [t[:, KD:KD + KC + 1] for t in terms]
        u_b = [sb("u0_b", [P, D]), sb("u1_b", [P, D])]
        bv0_b = sb("bv0_b", [P, D])
        gamma_b = sb("gamma_b", [P, D])
        beta_b = sb("beta_b", [P, D])
        gamma_col, bv1_col = sb("gamma_col", [P, KD]), sb("bv1_col", [P, KD])
        gscale = sb("gscale", [P, KD])

        XN = [sb("x_even", [P, J, D]), sb("x_odd", [P, J, D])]
        ctxn = sb("ctxn", [P, J, C])
        XT = pair("xT", [P, KD, J * P])
        Y = pair("y", [P, KC, J * P])
        E0 = sb("e0", [P, 2, RM, T])
        N = sb("n", [P, J, D])
        rs = sb("rs", [P, J])
        prod = [sb("prod0", [P, D]), sb("prod1", [P, D])]
        bias2 = sb("bias2", [P, D])
        w_lo_sum = Y[1][:, 0, :]
        r0 = sb("r0", [P, J])
        r0s = sb("r0s", [P, J])
        RB = sb("rb", [P, J * P])
        bias = [prod[0][:], prod[1][:], bias2[:], RB[:]]
        mx0, neg0, sum0, rinv0 = (sb(n, [P, J]) for n in ("mx0", "neg0", "sum0", "rinv0"))
        r1, mx1, top1, neg1, sum1, rinv1 = (sb(n, [P, J]) for n in ("r1", "mx1", "top1", "neg1", "sum1", "rinv1"))
        stats = sb("stats", [P, J, 6])
        mv = sb("mv", [P, J, 2])
        var_eps = sb("var_eps", [P, J])
        rstd = sb("rstd", [P, J])
        waited = sb("waited", [P, 2])
        minus_half = sb("minus_half", [P, J])
        CT_even, CN_even = pair("cT_even", [P, KC, J * P]), pair("cn_even", [P, J, C])

        with ExitStack() as stage0:
            wq0_sb = sb("wq0_sb", [P, KD, D], scope=stage0)
            wk0_sb = sb("wk0_sb", [P, KC, D], scope=stage0)
            wv0_sb = sb("wv0_sb", [P, KC, D], scope=stage0)
            wqT0 = sb("wqT0", [P, KD, D], scope=stage0)
            wkT0 = sb("wkT0", [P, KD, C], scope=stage0)
        CT_odd, CN_odd = pair("cT_odd", [P, KC, J * P]), pair("cn_odd", [P, J, C])
        W = pair("w", [P, 2, RM, T])
        WC = pair("wc", [P, 2, KC, T])
        CT, CN = [CT_even, CT_odd], [CN_even, CN_odd]
        with ExitStack() as stage1:
            wq1_sb = sb("wq1_sb", [P, KD, D], scope=stage1)
            wqT1 = sb("wqT1", [P, KD, D], scope=stage1)
            wk1_sb = sb("wk1_sb", [P, KC, D], scope=stage1)
            wkT1 = sb("wkT1", [P, KD, C], scope=stage1)
            wv1_sb = sb("wv1_sb", [P, KC, D], scope=stage1)
            wvT1 = sb("wvT1", [P, KD, C], scope=stage1)
            wo1_sb = sb("wo1_sb", [P, KD, D], scope=stage1)
            bo1_b = sb("bo1_b", [P, D], scope=stage1)
            bq0_b = sb("bq0_b", [P, D], scope=stage1)
            bk0_b = sb("bk0_b", [P, D], scope=stage1)
            bq1_b = sb("bq1_b", [P, D], scope=stage1)
            bk1_b = sb("bk1_b", [P, D], scope=stage1)
            betaq = sb("betaq", [P, KD], scope=stage1)
            dots = [sb(f"dots{n}", [P, KD + KC + 1], scope=stage1) for n in range(2)]
        NT = pair("nT", [P, KD, J * P])
        Y1 = pair("y1", [P, KC, J * P])
        PT = pair("pt", [P, 2, RM, T])
        PC = pair("pc", [P, 2, KC, T])
        E1 = sb("e1", [P, 2, RT, M])
        R = sb("r", [P, J, D])

        filled = [sem(f"filled{b}") for b in range(BANKS)]
        emptied = [sem(f"emptied{b}") for b in range(BANKS)]
        x_loaded = [sem("x_even_loaded"), sem("x_odd_loaded")]
        ctx_loaded = sem("ctx_loaded")
        last_stored = sem("last_stored")
        ROWS = 4
        rows_in_or_stored = sem("rows_in_or_stored")
        wq0_loaded = [sem(f"wq0_block{k}_loaded") for k in range(KD)]
        loaded = {n: sem(f"{n}_loaded") for n in
                  ("wk0", "wv0", "rows0", "rows1", "cols", "wq1", "wk1", "wv1", "wo1")}
        ident_ready, consts_ready, zeroed = sem("ident_ready"), sem("consts_ready"), sem("zeroed")
        wv0_hi, wv0_ready, gscale_ready = sem("wv0_rounded"), sem("wv0_ready"), sem("gscale_ready")
        dots_ready, u_ready, c_ready = sem("dots_ready"), sem("u_ready"), sem("c_ready")
        bvwo_ready, beta_added = sem("bvwo_ready"), sem("beta_added_to_bo")
        prep_hi = sem("prep_hi")
        hi = {n: sem(f"{n}_hi_ready") for n in ("xT", "cT", "cn", "y", "w", "wc", "nT", "y1", "pt", "pc")}
        cn_lo, w_lo, w_lo_added = sem("cn_lo_ready"), sem("w_lo_ready"), sem("w_lo_added")
        r0_ready, r0s_ready, exp0_ready = sem("r0_ready"), sem("r0s_ready"), sem("exp0_ready")
        mx0_ready, neg0_ready, rinv0_ready = sem("mx0_ready"), sem("neg0_ready"), sem("rinv0_ready")
        bias_ready, x_biased = sem("bias_ready"), sem("x_biased")
        stats_ready, mv_ready = sem("stats_ready"), sem("mv_ready")
        var_ready, rstd_ready, n_ready = sem("var_ready"), sem("rstd_ready"), sem("n_ready")
        prod_ready, r1_ready = sem("prod_ready"), sem("r1_ready")
        mx1_ready, top1_ready, neg1_ready, rinv1_ready = (sem("mx1_ready"), sem("top1_ready"),
                                                          sem("neg1_ready"), sem("rinv1_ready"))
        scaled_ready, resid_ready = sem("scaled_ready"), sem("resid_ready")

        block = whole.enter_context(nc.Block())

        def at(tile):
            return psum[BANK[tile]]

        def wait_filled(eng, it, name, k=0):
            eng.wait_ge(filled[BANK[name, k]], it.fill((name, k)))

        def wait_emptied(eng, it, name, k=0):
            eng.wait_ge(emptied[BANK[name, k]], it.fill((name, k)))

        before_last = Iteration(PAIRS, PAIRS - 1)

        def residual_of(it):
            return XN[1 - before_last.parity] if it.last else R

        def run(eng, iteration):
            iteration(Iteration(PAIRS, 0))
            with eng.Fori(0, (PAIRS - 2) // 2) as j:
                iteration(Iteration(PAIRS, 1, j))
                iteration(Iteration(PAIRS, 2, j))
            iteration(Iteration(PAIRS, PAIRS - 1))
            iteration(Iteration(PAIRS, PAIRS))

        @block.sync
        def _(sp):
            def known_early(it, value):
                if it.j is not None:
                    sp.compute_val(value)
                return value

            def rows_of(t, start):
                return t[bass.ds(start, J * P), :].rearrange("(j p) d -> p j d", p=P)

            def by_partition(v):
                return v.rearrange("(k p) -> p k", p=P)

            for k in range(KD):
                sp.dma_start(wq0_sb[:, k, :], wq0[k * P:(k + 1) * P, :]).then_inc(wq0_loaded[k], 16)
            sp.dma_start(wk0_sb[:], wk0.rearrange("(k p) e -> p k e", p=P)).then_inc(loaded["wk0"], 16)
            for t, v in ((bq0_b, bq0), (bk0_b, bk0)):
                sp.dma_start(t[:], v.partition_broadcast(P)).then_inc(loaded["rows0"], 16)
            sp.dma_start(XN[0][:], rows_of(x_rows, 0)).then_inc(x_loaded[0], 16)
            sp.dma_start(ctxn[:], rows_of(ctx_rows, 0)).then_inc(ctx_loaded, 16)
            sp.dma_start(wv0_sb[:], wv0.rearrange("(k p) e -> p k e", p=P)).then_inc(loaded["wv0"], 16)
            for t, v in ((bv0_b, bv0), (gamma_b, gamma), (beta_b, beta), (bo1_b, bo1)):
                sp.dma_start(t[:], v.partition_broadcast(P)).then_inc(rows_in_or_stored, 16)
            sp.dma_start(wq1_sb[:], wq1.rearrange("(k p) e -> p k e", p=P)).then_inc(loaded["wq1"], 16)
            for t, v in ((bq1_b, bq1), (bk1_b, bk1)):
                sp.dma_start(t[:], v.partition_broadcast(P)).then_inc(loaded["rows1"], 16)
            with nc.allow_non_contiguous_dma("two vectors, one element per partition"):
                for t, v in ((gamma_col, gamma), (bv1_col, bv1)):
                    sp.dma_start(t[:], by_partition(v)).then_inc(loaded["cols"], 16)
            sp.dma_start(wk1_sb[:], wk1.rearrange("(k p) e -> p k e", p=P)).then_inc(loaded["wk1"], 16)
            sp.dma_start(wv1_sb[:], wv1.rearrange("(k p) e -> p k e", p=P)).then_inc(loaded["wv1"], 16)
            sp.dma_start(wo1_sb[:], wo1.rearrange("(k p) e -> p k e", p=P)).then_inc(loaded["wo1"], 16)

            def iteration(it):
                more = it.j is not None or it.known < PAIRS - 1
                if more:
                    upcoming = known_early(it, it.times(J * P, J * P))
                    cT_filled = known_early(it, it.fill(("cT", KC - 1)))
                    cn_cut = known_early(it, it.times(1, 1))
                if it.back and not it.last:
                    finished = known_early(it, it.times(J * P, -J * P))
                    n_made = known_early(it, it.times(J, 0))
                    out_made = [known_early(it, it.fill(("out", j))) for j in range(J)]
                if more:
                    if it.back:
                        sp.wait_ge(n_ready, n_made)
                    sp.dma_start(XN[1 - it.parity][:], rows_of(x_rows, upcoming))\
                        .then_inc(x_loaded[1 - it.parity], 16)
                    sp.wait_ge(filled[BANK["cT", KC - 1]], cT_filled)
                    sp.wait_ge(cn_lo, cn_cut)
                    sp.dma_start(ctxn[:], rows_of(ctx_rows, upcoming)).then_inc(ctx_loaded, 16)
                if it.back and not it.before_last and not it.last:
                    for j in range(J):
                        sp.wait_ge(emptied[BANK["out", j]], out_made[j])
                    sp.dma_start(rows_of(out_rows, finished), R[:]).then_inc(rows_in_or_stored, 16)
                if it.last:
                    for j in range(J):
                        wait_emptied(sp, *((it, "late", j) if j in LATE else (before_last, "out", j)))
                    sp.dma_start(rows_of(out_rows, (PAIRS - 2) * J * P), R[:]).then_inc(rows_in_or_stored, 16)
                    for j in range(J):
                        wait_emptied(sp, it, "out", j)
                        start = ((PAIRS - 1) * J + j) * P
                        sp.dma_start(out_rows[start:start + P, :], residual_of(it)[:, j, :]).then_inc(last_stored, 16)

            run(sp, iteration)
            sp.wait_ge(rows_in_or_stored, 16 * (ROWS + PAIRS - 1))
            sp.wait_ge(last_stored, 16 * J)

        @block.tensor
        def _(pe):
            def begin(it, name, k=0):
                n = it.fill((name, k))
                if it.j is not None or n > 1:
                    pe.wait_ge(emptied[BANK[name, k]], n - 1)
                return at((name, k))

            def end(mm, name, k=0):
                mm.then_inc(filled[BANK[name, k]], 1)

            def passes(w, m):
                return ((w[0], m[0]), (w[0], m[1]), (w[1], m[0]))

            def product(dst, terms, last=True, first=True):
                for n, (w, m) in enumerate(terms):
                    mm = pe.matmul(dst, w, m, start=first and n == 0, stop=last and n == len(terms) - 1)
                return mm

            def transposes(it, name, k, blocks):
                dst = begin(it, name, k)
                for n, src in enumerate(blocks):
                    mm = pe.transpose(dst[:, n * P:(n + 1) * P], src, ident[:])
                end(mm, name, k)

            def weight_products(it, L, wqT, wkT):
                for k in range(KD):
                    g, h = divmod(k, 2)
                    if h == 0:
                        dst = begin(it, f"wqk{L}", g)
                    for e in range(KD):
                        if k == 0:
                            wait_emptied(pe, it, f"wqT{L}", e)
                            wait_emptied(pe, it, f"wkT{L}", e // 2)
                        mm = pe.matmul(dst[:, h * C:(h + 1) * C], wqT[:, e, k * P:(k + 1) * P], wkT[:, e, :],
                                       start=e == 0, stop=e == KD - 1)
                    if h == 1:
                        end(mm, f"wqk{L}", g)

            def spread(it, name, columns):
                transposes(it, name, 0, [columns[:, k:k + 1].to_broadcast([P, P]) for k in range(KD)])

            def transpose_kv(it, name, w, arrived):
                pe.wait_ge(arrived, 16)
                for g in range(2):
                    transposes(it, name, g, [w[:, c, e * P:(e + 1) * P]
                                             for e in (2 * g, 2 * g + 1) for c in range(KC)])

            def warm_up():
                for _ in range(5):
                    pe.matmul(psum[0][:], ones_r[:], ones_r[:, 0:1].to_broadcast([P, 512]), start=True, stop=True)

            def prepare0(it):
                pe.wait_ge(ident_ready, 2)
                for k in range(KD):
                    pe.wait_ge(wq0_loaded[k], 16)
                    for e in range(KD):
                        mm = pe.transpose(at(("wqT0", e))[:, k * P:(k + 1) * P], wq0_sb[:, k, e * P:(e + 1) * P],
                                          ident[:])
                        if k == KD - 1:
                            end(mm, "wqT0", e)
                transpose_kv(it, "wkT0", wk0_sb, loaded["wk0"])
                weight_products(it, 0, wqT0, wkT0)
                pe.wait_ge(u_ready, 1)
                spread(it, "u0", terms[0])

            def prepare1a(it):
                pe.wait_ge(loaded["wq1"], 16)
                for e in range(KD):
                    transposes(it, "wqT1", e, [wq1_sb[:, k, e * P:(e + 1) * P] for k in range(KD)])
                transpose_kv(it, "wkT1", wk1_sb, loaded["wk1"])

            def prepare1b(it):
                transpose_kv(it, "wvT1", wv1_sb, loaded["wv1"])
                weight_products(it, 1, wqT1, wkT1)
                pe.wait_ge(dots_ready, (KD + KC + 1) + KD)
                spread(it, "q1", betaq)
            def prepare1c(it):
                pe.wait_ge(u_ready, 2)
                spread(it, "u1", terms[1])
                for g in range(2):
                    wait_emptied(pe, it, "wvT1", g)
                pe.wait_ge(loaded["wo1"], 16)
                for c in range(KC):
                    dst = begin(it, "wvo", c)
                    end(product(dst[:], [(wvT1[:, h, c * P:(c + 1) * P], wo1_sb[:, h, :])
                                         for h in range(KD)]), "wvo", c)
                    if c == 0:
                        pe.wait_ge(bvwo_ready, 3)
                        dst = begin(it, "bo1")
                        end(product(dst[:], [(ones_r[:].bitcast(F32), wq1_sb[:, 0, :])]), "bo1")

            def transpose_inputs(it):
                xn = XN[it.parity]
                pe.wait_ge(x_loaded[it.parity], it.loads())
                for k in range(KD):
                    transposes(it, "xT", k, [xn[:, j, k * P:(k + 1) * P] for j in range(J)])
                pe.wait_ge(ctx_loaded, it.times(16, 16))
                for c in range(KC):
                    transposes(it, "cT", c, [ctxn[:, j, c * P:(c + 1) * P] for j in range(J)])

            def transpose_n(it):
                pe.wait_ge(n_ready, it.times(J, 0))
                for k in range(KD):
                    transposes(it, "nT", k, [N[:, j, k * P:(k + 1) * P] for j in range(J)])

            def project(it, name, source, wqk, src):
                dst = [begin(it, name, c) for c in range(KC)]
                for k in range(KD):
                    wait_emptied(pe, it, source, k)
                    for c in range(KC):
                        w = [h[:, k, c * P:(c + 1) * P] for h in wqk]
                        mm = product(dst[c][:], passes(w, [h[:, k, :] for h in src]),
                                     first=k == 0, last=k == KD - 1)
                        if k == KD - 1:
                            end(mm, name, c)

            def spread_r0(it):
                pe.wait_ge(r0s_ready, it.times(1, 1))
                spread(it, "rb", r0s)

            def scores0(it):
                ct = CT[it.parity]
                for c in range(KC):
                    wait_emptied(pe, it, "y", c)
                for c in range(KC):
                    wait_emptied(pe, it, "cT", c)
                for b in range(2):
                    dst = begin(it, "s0", b)
                    for mt in range(RM):
                        m0 = b * M + mt * P
                        part = dst[:, mt * T:(mt + 1) * T]
                        terms = []
                        for c in range(KC):
                            terms += passes([h[:, c, m0:m0 + P] for h in ct],
                                            [h[:, c, b * T:(b + 1) * T] for h in Y])
                        mm = product(part, terms)
                    end(mm, "s0", b)

            def scores1(it):
                ct = CT[1 - it.parity]
                for c in range(KC):
                    wait_emptied(pe, it, "y1", c)
                for b in range(2):
                    dst = begin(it, "s1", b)
                    for tt in range(RT):
                        t0 = b * T + tt * P
                        terms = []
                        for c in range(KC):
                            terms += passes([h[:, c, t0:t0 + P] for h in Y1],
                                            [h[:, c, b * M:(b + 1) * M] for h in ct])
                        mm = product(dst[:, tt * M:(tt + 1) * M], terms)
                    end(mm, "s1", b)

            def weigh(it, name, b, cn, probs):
                dst = begin(it, name, b)
                for ct in range(KC):
                    terms = []
                    for mt in range(RM):
                        terms += passes([h[:, b * RM + mt, ct * P:(ct + 1) * P] for h in cn],
                                        [h[:, b, mt, :] for h in probs])
                    mm = product(dst[:, ct * T:(ct + 1) * T], terms)
                end(mm, name, b)

            def weigh0(it, b):
                pe.wait_ge(w_lo, it.times(2 * RM, (b + 1) * RM))
                if b == 0:
                    pe.wait_ge(cn_lo, it.times(1, 1))
                weigh(it, "wc", b, CN[it.parity], W)

            def row_sums(it):
                pe.wait_ge(w_lo_added, it.times(1, 1))
                dst = begin(it, "rs")
                end(product(dst[:], [(ones_r[:], W[0][:, :, mt, :]) for mt in range(RM)] + [(ones_r[:], w_lo_sum)]),
                    "rs")

            def transpose_probs(it, b):
                wait_emptied(pe, it, "s1", b)
                transposes(it, "pt", b, [E1[:, b, tt, mt * P:(mt + 1) * P] for mt in range(RM) for tt in range(RT)])

            def apply(it, name, j, source, left, right):
                b, tt = divmod(j, RT)
                if tt == 0:
                    wait_emptied(pe, before_last if name == "late" else it, source, b)
                dst = begin(it, name, j)
                terms = []
                for ct in range(KC):
                    terms += passes([h[:, b, ct, tt * P:(tt + 1) * P] for h in left], [h[:, ct, :] for h in right])
                end(product(dst[:], terms), name, j)

            def iteration(it):
                begin_it = it.j is None and it.known == 0
                if begin_it:
                    prepare0(it)
                if it.front:
                    transpose_inputs(it)
                    project(it, "y", "xT", WQK[0], XT)
                if begin_it:
                    prepare1a(it)
                if it.back:
                    transpose_n(it)
                if it.front:
                    spread_r0(it)
                    scores0(it)
                if begin_it:
                    prepare1b(it)
                if it.back:
                    project(it, "y1", "nT", WQK[1], NT)
                if it.last:
                    apply(it, "late", 2, "pc", PC, WVO)
                if it.front:
                    weigh0(it, 0)
                    row_sums(it)
                    weigh0(it, 1)
                if it.back:
                    scores1(it)
                if it.last:
                    apply(it, "late", 3, "pc", PC, WVO)
                if it.front:
                    if begin_it:
                        pe.wait_ge(wv0_ready, 1)
                    apply(it, "pr", 0, "wc", WC, WV0)
                    apply(it, "pr", 1, "wc", WC, WV0)
                if it.back:
                    transpose_probs(it, 0)
                    transpose_probs(it, 1)
                for b in range(2):
                    if it.front:
                        apply(it, "pr", 2 + b, "wc", WC, WV0)
                    if it.back:
                        wait_emptied(pe, it, "pt", b)
                        weigh(it, "pc", b, CN[1 - it.parity], PT)
                if begin_it:
                    prepare1c(it)
                if it.back:
                    for j in range(LATE[0] if it.before_last else J):
                        apply(it, "out", j, "pc", PC, WVO)

            pe.wait_ge(consts_ready, 1)
            warm_up()
            run(pe, iteration)

        @block.scalar
        def _(act):
            def round_bank(it, name, k, dst, bias=None):
                wait_filled(act, it, name, k)
                if bias is not None:
                    i = act.activation(dst, at((name, k))[:], ACT.Identity, bias=bias)
                else:
                    i = act.activation(dst, at((name, k))[:], ACT.Copy)
                i.then_inc(hi[name] if name in hi else prep_hi, 1)

            def copy_bank(it, name, k, dst):
                wait_filled(act, it, name, k)
                act.activation(dst, at((name, k))[:], ACT.Copy).then_inc(emptied[BANK[name, k]], 1)

            def two(t, g):
                return t[:, 2 * g:2 * g + 2, :].rearrange("p k c -> p (k c)")

            def round_weights(it, L, k, scale):
                g, h = divmod(k, 2)
                wait_filled(act, it, f"wqk{L}", g)
                act.activation(WQK[L][0][:, k, :], at((f"wqk{L}", g))[:, h * C:(h + 1) * C], ACT.Copy,
                               scale=scale).then_inc(prep_hi, 1)

            def prepare0(it):
                for e in (0, 2):
                    copy_bank(it, "wqT0", e, wqT0[:, e, :])
                copy_bank(it, "wkT0", 0, two(wkT0, 0))
                for k in range(KD):
                    round_weights(it, 0, k, SCALE)
                copy_bank(it, "u0", 0, u_b[0][:])
                act.wait_ge(c_ready, 1)

            def prepare1a(it):
                for e in range(KD):
                    copy_bank(it, "wqT1", e, wqT1[:, e, :])
                for g in range(2):
                    copy_bank(it, "wkT1", g, two(wkT1, g))

            def prepare1b(it):
                for g in range(2):
                    copy_bank(it, "wvT1", g, two(wvT1, g))
                act.wait_ge(gscale_ready, 1)
                for k in range(KD):
                    round_weights(it, 1, k, gscale[:, k:k + 1])

            def cut_v0(it):
                act.wait_ge(loaded["wv0"], 16)
                act.activation(WV0[0][:], wv0_sb[:], ACT.Copy).then_inc(wv0_hi, 1)

            def prepare1c(it):
                copy_bank(it, "u1", 0, u_b[1][:])
                act.wait_ge(c_ready, 2)
                for c in range(KC):
                    round_bank(it, "wvo", c, WVO[0][:, c, :])

            def softmax0(it):
                for b in range(2):
                    act.wait_ge(neg0_ready, it.times(2, b + 1))
                    for mt in range(RM):
                        q = b * RM + mt
                        e = act.activation(E0[:, b, mt, :], E0[:, b, mt, :], ACT.Exp,
                                           bias=neg0[:, q:q + 1], accum_out=sum0[:, q:q + 1])
                    e.then_inc(exp0_ready, 1)
                for b in range(2):
                    act.wait_ge(rinv0_ready, it.times(2, b + 1))
                    for mt in range(RM):
                        q = b * RM + mt
                        act.activation(W[0][:, b, mt, :], E0[:, b, mt, :], ACT.Copy,
                                       scale=rinv0[:, q:q + 1]).then_inc(hi["w"], 1)

            def softmax1(it):
                for b in range(2):
                    act.wait_ge(neg1_ready, it.times(2, b - 1))
                    for tt in range(RT):
                        q = b * RT + tt
                        e = act.activation(E1[:, b, tt, :], at(("s1", b))[:, tt * M:(tt + 1) * M], ACT.Exp,
                                           bias=neg1[:, q:q + 1], accum_out=sum1[:, q:q + 1])
                    e.then_inc(emptied[BANK["s1", b]], 1)

            def bias_of_rows(it, j):
                wait_emptied(act, it, "rs")
                act.activation(bias[j], bv0_b[:], ACT.Copy, scale=rs[:, j:j + 1]).then_inc(bias_ready, 1)

            def row_terms(it, blocks):
                for j in blocks:
                    act.wait_ge(prod_ready, it.times(J, j + 1 - J))
                    act.activation(prod[j % 2][:], prod[j % 2][:], ACT.Copy,
                                   accum_out=r1[:, j:j + 1]).then_inc(r1_ready, 1)

            def halves(t, b):
                return t[:, b].rearrange("p k t -> p (k t)")

            def iteration(it):
                begin_it = it.j is None and it.known == 0
                if begin_it:
                    prepare0(it)
                if it.front:
                    for k in range(KD):
                        round_bank(it, "xT", k, XT[0][:, k, :])
                    for c in range(KC):
                        round_bank(it, "cT", c, CT[it.parity][0][:, c, :])
                    act.wait_ge(ctx_loaded, it.times(16, 16))
                    act.activation(CN[it.parity][0][:], ctxn[:], ACT.Copy).then_inc(hi["cn"], 1)
                    if begin_it:
                        cut_v0(it)
                    for c in range(KC):
                        round_bank(it, "y", c, Y[0][:, c, :], bias=ccol[0][:, c:c + 1])
                if begin_it:
                    prepare1a(it)
                if it.back:
                    for k in range(KD):
                        round_bank(it, "nT", k, NT[0][:, k, :])
                if it.front:
                    copy_bank(it, "rb", 0, RB[:])
                if it.back:
                    row_terms(it, (0, 1))
                if it.front:
                    softmax0(it)
                if begin_it:
                    prepare1b(it)
                if it.back:
                    row_terms(it, (2, 3))
                    for c in range(KC):
                        round_bank(it, "y1", c, Y1[0][:, c, :], bias=ccol[1][:, c:c + 1])
                if it.front:
                    if begin_it:
                        act.wait_ge(rows_in_or_stored, 16 * ROWS)
                    for b in range(2):
                        round_bank(it, "wc", b, halves(WC[0], b))
                        bias_of_rows(it, b)
                    for j in range(2, J):
                        bias_of_rows(it, j)
                if it.back:
                    softmax1(it)
                if begin_it:
                    prepare1c(it)
                if it.back:
                    for b in range(2):
                        round_bank(it, "pt", b, halves(PT[0], b))
                    for b in range(2):
                        round_bank(it, "pc", b, halves(PC[0], b))

            run(act, iteration)

        @block.vector
        def _(dve):
            counted = {"prep": 0, "dots": 0}

            def low(it, name, k, dst, high, bias=None, per=0, back=0):
                dve.wait_ge(hi[name], it.times(per, k + 1 - back * per))
                src = at((name, k))[:]
                if bias is not None:
                    i = dve.scalar_tensor_tensor(dst, src, bias, high.bitcast(F32), ALU.add, ALU.subtract)
                else:
                    i = dve.tensor_tensor(dst, src, high.bitcast(F32), ALU.subtract)
                i.then_inc(emptied[BANK[name, k]], 1)

            def low_weights(it, name, k, parts, bank_parts, scales):
                counted["prep"] += len(parts)
                dve.wait_ge(prep_hi, counted["prep"])
                for (high, lo), src, scale in zip(parts, bank_parts, scales):
                    i = dve.scalar_tensor_tensor(lo, src, scale, high.bitcast(F32), ALU.mult, ALU.subtract)
                i.then_inc(emptied[BANK[name, k]], 1)

            def low_wqk(it, L, scale_of):
                for g in range(KD // 2):
                    bank = at((f"wqk{L}", g))
                    low_weights(it, f"wqk{L}", g, [[h[:, 2 * g + n, :] for h in WQK[L]] for n in range(2)],
                                [bank[:, n * C:(n + 1) * C] for n in range(2)],
                                [scale_of(2 * g + n) for n in range(2)])

            def dot(dst, a, b):
                n = counted["dots"]
                counted["dots"] += 1
                if n >= J:
                    dve.wait_ge(dots_ready, n - J + 1)
                i = dve.tensor_tensor_reduce(N[:, n % J, :], a, b, 1.0, 0.0, ALU.mult, ALU.add, dst)
                i.then_inc(dots_ready, 1)

            def dots_done():
                dve.wait_ge(dots_ready, counted["dots"])

            def wq_bk(L, wq, bk):
                for k in range(KD):
                    dot(dots[L][:, k:k + 1], wq[:, k, :], bk[:])

            def wk_bq(L, wk, bq, bk):
                for c in range(KC):
                    dot(dots[L][:, KD + c:KD + c + 1], wk[:, c, :], bq[:])
                dot(dots[L][:, KD + KC:], bk[:], bq[:])
                dots_done()
                dve.tensor_scalar(ccol[L], dots[L][:, KD:], SCALE, None, ALU.mult).then_inc(c_ready, 1)

            def prepare0(it):
                for e in (1, 3):
                    wait_filled(dve, it, "wqT0", e)
                    dve.tensor_copy(wqT0[:, e, :], at(("wqT0", e))[:]).then_inc(emptied[BANK["wqT0", e]], 1)
                wait_filled(dve, it, "wkT0", 1)
                dve.tensor_copy(wkT0[:, 2:4, :].rearrange("p k c -> p (k c)"), at(("wkT0", 1))[:])\
                   .then_inc(emptied[BANK["wkT0", 1]], 1)
                dve.wait_ge(loaded["rows0"], 16 * 2)
                dve.wait_ge(loaded["wk0"], 16)
                wk_bq(0, wk0_sb, bq0_b, bk0_b)
                for k in range(KD):
                    dve.wait_ge(wq0_loaded[k], 16)
                wq_bk(0, wq0_sb, bk0_b)
                dots_done()
                dve.tensor_scalar(terms[0][:, :KD], dots[0][:, :KD], SCALE, None, ALU.mult).then_inc(u_ready, 1)
                low_wqk(it, 0, lambda k: SCALE)

            def prepare1a(it):
                dve.wait_ge(loaded["cols"], 16 * 2)
                dve.tensor_scalar(gscale[:], gamma_col[:], SCALE, None, ALU.mult).then_inc(gscale_ready, 1)
                dve.wait_ge(rows_in_or_stored, 16 * ROWS)
                dve.tensor_tensor(bo1_b[:], bo1_b[:], beta_b[:], ALU.add).then_inc(beta_added, 1)

            def cut_v0(it):
                dve.wait_ge(wv0_hi, 1)
                dve.tensor_tensor(WV0[1][:], wv0_sb[:], WV0[0][:].bitcast(F32), ALU.subtract).then_inc(wv0_ready, 1)

            def row_terms1(it):
                dve.wait_ge(loaded["wq1"], 16)
                dve.wait_ge(loaded["rows1"], 16 * 2)
                wq_bk(1, wq1_sb, bk1_b)
                dots_done()
                dve.wait_ge(gscale_ready, 1)
                dve.tensor_tensor(terms[1][:, :KD], dots[1][:, :KD], gscale[:], ALU.mult).then_inc(u_ready, 1)
                wait_filled(dve, it, "q1")
                dve.tensor_tensor(bq1_b[:], at(("q1", 0))[:], bq1_b[:], ALU.add).then_inc(emptied[BANK["q1", 0]], 1)

            def beta_wq1(it):
                dve.wait_ge(rows_in_or_stored, 16 * ROWS)
                for e in range(KD):
                    wait_emptied(dve, it, "wqT1", e)
                    dot(betaq[:, e:e + 1], wqT1[:, e, :], beta_b[:])
                dots_done()

            def prepare1b(it):
                low_wqk(it, 1, lambda k: gscale[:, k:k + 1])

            def column_terms1(it):
                wait_emptied(dve, it, "q1")
                dve.wait_ge(loaded["wk1"], 16)
                wk_bq(1, wk1_sb, bq1_b, bk1_b)

            def finish_beta(it):
                dve.wait_ge(beta_added, 1)
                wait_filled(dve, it, "bo1")
                dve.tensor_tensor(beta_b[:], at(("bo1", 0))[:], bo1_b[:], ALU.add)\
                   .then_inc(emptied[BANK["bo1", 0]], 1)

            def prepare1c(it):
                for c in range(KC):
                    low_weights(it, "wvo", c, [[h[:, c, :] for h in WVO]], [at(("wvo", c))[:]], [1.0])

            def row_terms0(it):
                dve.wait_ge(x_loaded[it.parity], it.loads())
                if it.j is None and it.known == 0:
                    wait_emptied(dve, it, "u0")
                for j in range(J):
                    if it.j is not None or it.known or j:
                        dve.wait_ge(r0_ready, it.times(J, j))
                    dve.tensor_tensor_reduce(RB[:], XN[it.parity][:, j, :], u_b[0][:], 1.0, 0.0, ALU.mult,
                                             ALU.add, r0[:, j:j + 1]).then_inc(r0_ready, 1)
                dve.wait_ge(r0_ready, it.times(J, J))
                dve.tensor_scalar(r0s[:], r0[:], ccol[0][:, KC:KC + 1], None, ALU.add).then_inc(r0s_ready, 1)

            def maxima0(it):
                for b in range(2):
                    if b == 0:
                        wait_emptied(dve, it, "rb")
                    wait_filled(dve, it, "s0", b)
                    dve.memset(waited[:, b:b + 1], 0.0)
                    for mt in range(RM):
                        q = b * RM + mt
                        i = dve.tensor_tensor_reduce(E0[:, b, mt, :], at(("s0", b))[:, mt * T:(mt + 1) * T],
                                                     RB[:, b * T:(b + 1) * T], 1.0, LOWEST, ALU.add, ALU.max,
                                                     mx0[:, q:q + 1])
                        i.then_inc(*((emptied[BANK["s0", b]], 1) if mt == RM - 1 else (mx0_ready, 1)))
                    dve.wait_ge(mx0_ready, it.times(2, b + 1))
                    wait_emptied(dve, it, "s0", b)
                    q = slice(b * RM, (b + 1) * RM)
                    dve.tensor_scalar(neg0[:, q], mx0[:, q], -1.0, None, ALU.mult).then_inc(neg0_ready, 1)

            def maxima1(it):
                s = ccol[1][:, KC:KC + 1]
                dve.wait_ge(r1_ready, it.times(J, 0))
                for b in range(2):
                    wait_filled(dve, it, "s1", b)
                    q = slice(b * RT, (b + 1) * RT)
                    dve.tensor_reduce(mx1[:, q], at(("s1", b))[:].rearrange("p (t m) -> p t m", t=RT), AX_X,
                                      ALU.max).then_inc(mx1_ready, 1)
                    dve.wait_ge(mx1_ready, it.times(2, b - 1))
                    dve.scalar_tensor_tensor(top1[:, q], r1[:, q], s, mx1[:, q], ALU.add, ALU.add)\
                       .then_inc(top1_ready, 1)
                    dve.wait_ge(top1_ready, it.times(2, b - 1))
                    dve.scalar_tensor_tensor(neg1[:, q], r1[:, q], s, top1[:, q], ALU.add, ALU.subtract)\
                       .then_inc(neg1_ready, 1)

            def normalise0(it):
                for b in range(2):
                    dve.wait_ge(exp0_ready, it.times(2, b + 1))
                    q = slice(b * RM, (b + 1) * RM)
                    dve.reciprocal(rinv0[:, q], sum0[:, q]).then_inc(rinv0_ready, 1)
                for b in range(2):
                    for mt in range(RM):
                        q = b * RM + mt
                        dve.wait_ge(hi["w"], it.times(2 * RM, q + 1))
                        dve.scalar_tensor_tensor(W[1][:, b, mt, :], E0[:, b, mt, :], rinv0[:, q:q + 1],
                                                 W[0][:, b, mt, :].bitcast(F32), ALU.mult, ALU.subtract)\
                           .then_inc(w_lo, 1)

            def output(it, j, name="out", pair_of=None):
                wait_filled(dve, it, name, j)
                dve.wait_ge(resid_ready, (pair_of or it).times(J, j + 1 - J))
                r = residual_of(pair_of or it)
                dve.scalar_tensor_tensor(r[:, j, :], at((name, j))[:], rinv1[:, j:j + 1], r[:, j, :],
                                         ALU.mult, ALU.add).then_inc(emptied[BANK[name, j]], 1)

            def norm_and_output(it):
                xn = XN[it.parity]

                def add(j):
                    wait_filled(dve, it, "pr", j)
                    dve.wait_ge(x_biased, it.times(J, j + 1))
                    dve.tensor_tensor(xn[:, j, :], at(("pr", j))[:], xn[:, j, :], ALU.add)\
                       .then_inc(emptied[BANK["pr", j]], 1)

                def statistics(j):
                    wait_emptied(dve, it, "pr", j)
                    dve.bn_stats(stats[:, j, :], xn[:, j, :]).then_inc(stats_ready, 1)

                def aggregate(b):
                    for j in range(b * RT, (b + 1) * RT):
                        dve.bn_aggr(mv[:, j, :], stats[:, j, :]).then_inc(mv_ready, 1)
                    dve.wait_ge(mv_ready, it.times(J, (b + 1) * RT))
                    q = slice(b * RT, (b + 1) * RT)
                    dve.tensor_scalar(var_eps[:, q], mv[:, q, 1], EPS, None, ALU.add).then_inc(var_ready, 1)

                def normalise(j):
                    dve.wait_ge(rstd_ready, it.times(2, j // RT + 1))
                    dve.tensor_scalar(N[:, j, :], xn[:, j, :], mv[:, j, 0:1], rstd[:, j:j + 1], ALU.subtract,
                                      ALU.mult).then_inc(n_ready, 1)

                def cut_pc(b):
                    low(it, "pc", b, halves(PC[1], b), halves(PC[0], b), per=2, back=1)

                def cut_pt(b):
                    low(it, "pt", b, halves(PT[1], b), halves(PT[0], b), per=2, back=1)

                if it.front:
                    add(0)
                    statistics(0)
                    add(1)
                if it.back:
                    cut_pt(0)
                    cut_pt(1)
                if it.front:
                    statistics(1)
                if it.back:
                    wait_emptied(dve, it, "s1", 1)
                    if it.last:
                        wait_emptied(dve, it, "late", 3)
                    dve.reciprocal(rinv1[:], sum1[:]).then_inc(rinv1_ready, 1)
                if it.front:
                    dve.wait_ge(stats_ready, it.times(J, RT))
                    add(2)
                    aggregate(0)
                    statistics(2)
                if it.back:
                    cut_pc(0)
                if it.front:
                    if it.back:
                        wait_filled(dve, it, "nT", KD - 1)
                        dve.wait_ge(scaled_ready, it.times(J, 0))
                    normalise(0)
                    normalise(1)
                    add(3)
                    statistics(3)
                if it.before_last:
                    dve.wait_ge(stats_ready, it.times(J, J))
                    aggregate(1)
                if it.back:
                    cut_pc(1)
                if it.before_last:
                    normalise(2)
                    normalise(3)
                if it.back:
                    dve.wait_ge(rinv1_ready, it.times(1, 0))
                    output(it, 0)
                    if it.front and not it.before_last:
                        dve.wait_ge(stats_ready, it.times(J, J))
                    output(it, 1)
                if it.front and not it.before_last:
                    if not it.back:
                        dve.wait_ge(stats_ready, it.times(J, J))
                    aggregate(1)
                    if not it.back:
                        finish_beta(it)
                if it.back and not it.before_last:
                    output(it, 2)
                if it.front and not it.before_last:
                    normalise(2)
                    normalise(3)
                if it.back and not it.before_last:
                    output(it, 3)

            def halves(t, b):
                return t[:, b].rearrange("p k t -> p (k t)")

            def iteration(it):
                begin_it = it.j is None and it.known == 0
                if begin_it:
                    prepare0(it)
                if it.front:
                    for k in range(KD):
                        low(it, "xT", k, XT[1][:, k, :], XT[0][:, k, :], per=KD)
                    for c in range(KC):
                        low(it, "cT", c, CT[it.parity][1][:, c, :], CT[it.parity][0][:, c, :], per=KC)
                    row_terms0(it)
                    for c in range(KC):
                        low(it, "y", c, Y[1][:, c, :], Y[0][:, c, :], bias=ccol[0][:, c:c + 1], per=KC)
                if begin_it:
                    prepare1a(it)
                    cut_v0(it)
                if it.back:
                    for k in range(KD):
                        low(it, "nT", k, NT[1][:, k, :], NT[0][:, k, :], per=KD, back=1)
                if it.front:
                    maxima0(it)
                if begin_it:
                    beta_wq1(it)
                if it.front:
                    normalise0(it)
                if begin_it:
                    row_terms1(it)
                if it.back:
                    for c in range(KC):
                        low(it, "y1", c, Y1[1][:, c, :], Y1[0][:, c, :], bias=ccol[1][:, c:c + 1], per=KC, back=1)
                if it.front:
                    wait_filled(dve, it, "rs")
                    for j in range(J):
                        q = slice(j * P, (j + 1) * P)
                        i = dve.tensor_tensor_reduce(halves(E0, 0)[:, q], at(("rs", 0))[:, q], ident[:], 1.0, 0.0,
                                                     ALU.mult, ALU.add, rs[:, j:j + 1])
                    i.then_inc(emptied[BANK["rs", 0]], 1)
                    for b in range(2):
                        low(it, "wc", b, halves(WC[1], b), halves(WC[0], b), per=2)
                if begin_it:
                    prepare1b(it)
                    column_terms1(it)
                if it.last:
                    output(it, 2, "late", before_last)
                if it.back:
                    maxima1(it)
                if it.last:
                    output(it, 3, "late", before_last)
                norm_and_output(it)
                if begin_it:
                    prepare1c(it)

            run(dve, iteration)

        @block.gpsimd
        def _(pool):
            pool.memset(ones_r[:].bitcast(F32), 1.0).then_inc(consts_ready, 1)
            pool.memset(ident[:], 0.0).then_inc(ident_ready, 1)
            pool.wait_ge(ident_ready, 1)
            pool.affine_select(out=ident[:], in_=ident[:], compare_op=ALU.not_equal, fill=1.0, base=0,
                               pattern=[[-1, P]], channel_multiplier=1).then_inc(ident_ready, 1)
            pool.memset(minus_half[:], -0.5).then_inc(consts_ready, 1)
            pool.wait_ge(consts_ready, 2)

            def cut_ctx(it):
                pool.wait_ge(hi["cn"], it.times(1, 1))
                pool.tensor_tensor(CN[it.parity][1][:], ctxn[:], CN[it.parity][0][:].bitcast(F32), ALU.subtract)\
                    .then_inc(cn_lo, 1)

            def bv_wo():
                pool.wait_ge(loaded["wo1"], 16)
                pool.wait_ge(loaded["cols"], 16 * 2)
                pool.wait_ge(u_ready, 2)
                pool.tensor_tensor(wq1_sb[:], wo1_sb[:], bv1_col[:].unsqueeze(2).to_broadcast([P, KD, D]), ALU.mult)\
                    .then_inc(bvwo_ready, 1)
                for half in (2, 1):
                    pool.wait_ge(bvwo_ready, 3 - half)
                    pool.tensor_tensor(wq1_sb[:, 0:half, :], wq1_sb[:, 0:half, :], wq1_sb[:, half:2 * half, :],
                                       ALU.add).then_inc(bvwo_ready, 1)

            def rstds(it):
                for b in range(2):
                    pool.wait_ge(var_ready, it.times(2, b + 1))
                    q = slice(b * RT, (b + 1) * RT)
                    pool.tensor_tensor(rstd[:, q], var_eps[:, q], minus_half[:, q], ALU.pow).then_inc(rstd_ready, 1)

            def row_products(it, blocks):
                for j in blocks:
                    pool.wait_ge(n_ready, it.times(J, j + 1 - J))
                    if j >= 2:
                        pool.wait_ge(r1_ready, it.times(J, j - 1 - J))
                    pool.tensor_tensor(prod[j % 2][:], N[:, j, :], u_b[1][:], ALU.mult).then_inc(prod_ready, 1)

            def add_w_lo(it):
                pool.wait_ge(w_lo, it.times(2 * RM, 2 * RM))
                pool.tensor_tensor(w_lo_sum.rearrange("p (b t) -> p b t", b=2), W[1][:, :, 0, :].bitcast(F32),
                                   W[1][:, :, 1, :].bitcast(F32), ALU.add).then_inc(w_lo_added, 1)

            def add_bias(it):
                xn = XN[it.parity]
                for j in range(J):
                    pool.wait_ge(bias_ready, it.times(J, j + 1))
                    pool.tensor_tensor(xn[:, j, :], bias[j], xn[:, j, :], ALU.add).then_inc(x_biased, 1)

            def scale_n(it):
                if not it.last:
                    pool.wait_ge(rows_in_or_stored, it.times(16, 16 * (ROWS - 1)))
                r = residual_of(it)
                for j in range(J):
                    pool.wait_ge(n_ready, it.times(J, j + 1 - J))
                    pool.tensor_tensor(r[:, j, :], N[:, j, :], gamma_b[:], ALU.mult).then_inc(scaled_ready, 1)

            def add_beta(it, blocks):
                r = residual_of(it)
                for j in blocks:
                    pool.wait_ge(scaled_ready, it.times(J, j + 1 - J))
                    pool.tensor_tensor(r[:, j, :], r[:, j, :], beta_b[:], ALU.add).then_inc(resid_ready, 1)

            def iteration(it):
                if it.front:
                    cut_ctx(it)
                if it.back:
                    row_products(it, (0, 1))
                    if it.front:
                        scale_n(it)
                    row_products(it, (2, 3))
                    if not it.front:
                        scale_n(it)
                if it.front:
                    add_w_lo(it)
                if it.back:
                    add_beta(it, (0, 1))
                if it.j is None and it.known == 0:
                    bv_wo()
                if it.front:
                    add_bias(it)
                if it.back:
                    add_beta(it, (2, 3))
                if it.front:
                    rstds(it)

            def guarded(it):
                if it.j is None and it.known == 0:
                    iteration(it)
                    wait_emptied(pool, it, "u1")
                    wait_emptied(pool, it, "bo1")
                else:
                    iteration(it)

            run(pool, guarded)


_INS = ['x', 'ctx_512', 'L0_xattn_Wq', 'L0_xattn_bq', 'L0_xattn_Wk', 'L0_xattn_bk', 'L0_xattn_Wv', 'L0_xattn_bv',
        'L0_xattn_gamma', 'L0_xattn_beta', 'L1_xattn_Wq', 'L1_xattn_bq', 'L1_xattn_Wk', 'L1_xattn_bk',
        'L1_xattn_Wv', 'L1_xattn_bv', 'L1_xattn_Wo', 'L1_xattn_bo']


def kernel(**inputs):
    import numpy as _np
    import concourse.bacc as _bacc
    from concourse import mybir as _mybir
    from concourse.bass_utils import run_bass_kernel_spmd as _run

    nc = _bacc.Bacc("TRN2", target_bir_lowering=False, num_devices=1)
    arrays, args = {}, []
    for name in _INS:
        a = _np.ascontiguousarray(inputs[name])
        arrays[f"in_{name}_dram"] = a
        args.append(nc.dram_tensor(f"in_{name}_dram", a.shape, _mybir.dt.from_np(a.dtype), kind="ExternalInput").ap())
    args.append(nc.dram_tensor("out_0_dram", inputs['x'].shape, _mybir.dt.float32, kind="ExternalOutput").ap())
    two_cross_attentions(nc, *args)
    r = _run(nc, [arrays], core_ids=[0])
    return r.results[0]["out_0_dram"]
```
